# Optimizing a Trainium2 kernel written in Bass

```python
import numpy as np
import jax
import jax.numpy as jnp

def _softmax(x, axis=-1):
    return jax.nn.softmax(x, axis=axis)

def _gelu(x):
    return jax.nn.gelu(x, approximate=True)

def _silu(x):
    return jax.nn.silu(x)

def _sigmoid(x):
    return jax.nn.sigmoid(x)

def _layernorm(x, axis=-1, eps=1e-05):
    m = jnp.mean(x, axis=axis, keepdims=True)
    v = jnp.var(x, axis=axis, keepdims=True)
    return (x - m) / jnp.sqrt(v + eps)

def _scatter_add(tgt, idx, src, axis=0):
    return tgt.at[idx].add(src)

def _segment_sum(src, seg, n):
    return jax.ops.segment_sum(src, seg, n)
kernel_name = 'mk_gnn_resnorm_d1_gnn_r8_2b60a8'

def setup_inputs(seed: int=0):
    np.random.seed(seed)
    _w = jnp.asarray

    def _rec_inputs():
        import jax
        import jax.numpy as jnp
        _gk = jax.random.key(seed)
        x = -8.776e-05 + 1 * jax.random.normal(jax.random.fold_in(_gk, 1), (1250, 512), jnp.float32)
        src = jax.random.randint(jax.random.fold_in(_gk, 2), (40000,), 0, 1250, jnp.int32)
        dst = jax.random.randint(jax.random.fold_in(_gk, 3), (40000,), 0, 1250, jnp.int32)
        _o = jnp.argsort(dst, stable=True)
        src = src[_o]
        dst = dst[_o]
        edge_attr_3 = -0.000369394 + 0.57735 * jax.random.normal(jax.random.fold_in(_gk, 11), (40000, 3), jnp.float32)
        edge_weight = jax.random.uniform(jax.random.fold_in(_gk, 13), (40000,), jnp.float32, 0.0, 1.39999)
        return (x, src, dst, edge_attr_3, edge_weight)
    x, src, dst, edge_attr_3, edge_weight = _rec_inputs()

    def _L0_gnn_setup():
        import jax, jax.numpy as jnp
        import numpy as np
        N_NODES = 1250
        N_EDGES = 20000
        R_CUT = 1.4415
        N_RBF = 20

        def silu(x):
            return x * jax.nn.sigmoid(x)

        def _painn_block(x, edge_index, edge_attr1, edge_attr2, W1, b1, W2, b2, W3, b3, U, V, Wu1, bu1, Wu2, bu2):
            src, dst = (edge_index[0], edge_index[1])
            E = src.shape[0]
            x_j = x[src]
            v_j = x_j[:, :384].reshape(E, 128, 3)
            s_j = x_j[:, 384:]
            s_j = silu(s_j @ W1 + b1) @ W3 + b3
            r = edge_attr2[:, None]
            n = jnp.arange(1, N_RBF + 1, dtype=x.dtype)
            rbf = jnp.sqrt(2.0 / R_CUT) * jnp.sin(n * jnp.pi * r / R_CUT) / r
            cutoff = 0.5 * (jnp.cos(jnp.pi * r / R_CUT) + 1.0) * (r < R_CUT)
            edge_basis = rbf * cutoff @ W2 + b2
            split = s_j * edge_basis
            s1, s2, s3 = (split[:, :128], split[:, 128:256], split[:, 256:])
            v_msg = v_j * s1[:, :, None] + s3[:, :, None] * edge_attr1[:, None, :]
            msg = jnp.concatenate([v_msg.reshape(E, 384), s2], axis=1)
            x = x + jax.ops.segment_sum(msg, dst, num_segments=N_NODES)
            x_j = x[src]
            v = x_j[:, :384].reshape(E, 3, 128)
            v = v @ U
            v_V = v @ V
            v = v.reshape(E, 128, 3)
            v_V = v_V.reshape(E, 128, 3)
            norm = jnp.linalg.norm(v_V, axis=2)
            s = x_j[:, 384:]
            h = silu(jnp.concatenate([norm, s], axis=1) @ Wu1 + bu1) @ Wu2 + bu2
            s1, s2, s3 = (h[:, :128], h[:, 128:256], h[:, 256:])
            v = v * s1[:, :, None]
            dot = jnp.einsum('ijk,ijk->ij', v, v_V)
            scal = dot + s3
            msg = jnp.concatenate([v.reshape(E, 384), scal], axis=1)
            x = x + jax.ops.segment_sum(msg, dst, num_segments=N_NODES)
            return x
        key = jax.random.key(seed)
        ks = jax.random.split(key, 12)
        x = jax.random.normal(ks[0], (N_NODES, 512), jnp.float32)
        edge_index = jax.random.randint(ks[1], (2, N_EDGES), 0, N_NODES, dtype=jnp.int64)
        ea1 = jax.random.normal(ks[2], (N_EDGES, 3), jnp.float32)
        edge_attr1 = ea1 / jnp.linalg.norm(ea1, axis=1, keepdims=True)
        edge_attr2 = jax.random.uniform(ks[3], (N_EDGES,), jnp.float32) * 1.3 + 0.1

        def lin(k, fi, fo):
            return (jax.random.normal(k, (fi, fo), jnp.float32) / np.sqrt(fi)).astype(jnp.float32)
        return {'x': x, 'edge_index': edge_index, 'edge_attr1': edge_attr1, 'edge_attr2': edge_attr2, 'W1': lin(ks[4], 128, 128), 'b1': jnp.zeros(128, jnp.float32), 'W2': lin(ks[5], 20, 384), 'b2': jnp.zeros(384, jnp.float32), 'W3': lin(ks[6], 128, 384), 'b3': jnp.zeros(384, jnp.float32), 'U': lin(ks[7], 128, 128), 'V': lin(ks[8], 128, 128), 'Wu1': lin(ks[9], 256, 128), 'bu1': jnp.zeros(128, jnp.float32), 'Wu2': lin(ks[10], 128, 384), 'bu2': jnp.zeros(384, jnp.float32)}
    _L0_gnn_all = _L0_gnn_setup()
    _L0_gnn_in = {k: v for k, v in _L0_gnn_all.items() if k in ('W1', 'b1', 'W2', 'b2', 'W3', 'b3', 'U', 'V', 'Wu1', 'bu1', 'Wu2', 'bu2')}
    del _L0_gnn_all
    return {'x': x, 'src': src, 'dst': dst, 'edge_attr_3': edge_attr_3, 'edge_weight': edge_weight, 'L0_gnn_W1': _L0_gnn_in['W1'], 'L0_gnn_b1': _L0_gnn_in['b1'], 'L0_gnn_W2': _L0_gnn_in['W2'], 'L0_gnn_b2': _L0_gnn_in['b2'], 'L0_gnn_W3': _L0_gnn_in['W3'], 'L0_gnn_b3': _L0_gnn_in['b3'], 'L0_gnn_U': _L0_gnn_in['U'], 'L0_gnn_V': _L0_gnn_in['V'], 'L0_gnn_Wu1': _L0_gnn_in['Wu1'], 'L0_gnn_bu1': _L0_gnn_in['bu1'], 'L0_gnn_Wu2': _L0_gnn_in['Wu2'], 'L0_gnn_bu2': _L0_gnn_in['bu2']}

def reference(x, src, dst, edge_attr_3, edge_weight, L0_gnn_W1, L0_gnn_b1, L0_gnn_W2, L0_gnn_b2, L0_gnn_W3, L0_gnn_b3, L0_gnn_U, L0_gnn_V, L0_gnn_Wu1, L0_gnn_bu1, L0_gnn_Wu2, L0_gnn_bu2):
    import jax
    import jax.numpy as jnp

    def _L0_gnn_ref(x, edge_index, edge_attr1, edge_attr2, W1, b1, W2, b2, W3, b3, U, V, Wu1, bu1, Wu2, bu2):
        import jax, jax.numpy as jnp
        import numpy as np
        N_NODES = 1250
        N_EDGES = 20000
        R_CUT = 1.4415
        N_RBF = 20

        def silu(x):
            return x * jax.nn.sigmoid(x)

        def _painn_block(x, edge_index, edge_attr1, edge_attr2, W1, b1, W2, b2, W3, b3, U, V, Wu1, bu1, Wu2, bu2):
            src, dst = (edge_index[0], edge_index[1])
            E = src.shape[0]
            x_j = x[src]
            v_j = x_j[:, :384].reshape(E, 128, 3)
            s_j = x_j[:, 384:]
            s_j = silu(s_j @ W1 + b1) @ W3 + b3
            r = edge_attr2[:, None]
            n = jnp.arange(1, N_RBF + 1, dtype=x.dtype)
            rbf = jnp.sqrt(2.0 / R_CUT) * jnp.sin(n * jnp.pi * r / R_CUT) / r
            cutoff = 0.5 * (jnp.cos(jnp.pi * r / R_CUT) + 1.0) * (r < R_CUT)
            edge_basis = rbf * cutoff @ W2 + b2
            split = s_j * edge_basis
            s1, s2, s3 = (split[:, :128], split[:, 128:256], split[:, 256:])
            v_msg = v_j * s1[:, :, None] + s3[:, :, None] * edge_attr1[:, None, :]
            msg = jnp.concatenate([v_msg.reshape(E, 384), s2], axis=1)
            x = x + jax.ops.segment_sum(msg, dst, num_segments=N_NODES)
            x_j = x[src]
            v = x_j[:, :384].reshape(E, 3, 128)
            v = v @ U
            v_V = v @ V
            v = v.reshape(E, 128, 3)
            v_V = v_V.reshape(E, 128, 3)
            norm = jnp.linalg.norm(v_V, axis=2)
            s = x_j[:, 384:]
            h = silu(jnp.concatenate([norm, s], axis=1) @ Wu1 + bu1) @ Wu2 + bu2
            s1, s2, s3 = (h[:, :128], h[:, 128:256], h[:, 256:])
            v = v * s1[:, :, None]
            dot = jnp.einsum('ijk,ijk->ij', v, v_V)
            scal = dot + s3
            msg = jnp.concatenate([v.reshape(E, 384), scal], axis=1)
            x = x + jax.ops.segment_sum(msg, dst, num_segments=N_NODES)
            return x
        return _painn_block(x, edge_index, edge_attr1, edge_attr2, W1, b1, W2, b2, W3, b3, U, V, Wu1, bu1, Wu2, bu2)
    edge_index = jnp.stack([src, dst])
    x = _layernorm(x + _L0_gnn_ref(x, edge_index, edge_attr_3, edge_weight, L0_gnn_W1, L0_gnn_b1, L0_gnn_W2, L0_gnn_b2, L0_gnn_W3, L0_gnn_b3, L0_gnn_U, L0_gnn_V, L0_gnn_Wu1, L0_gnn_bu1, L0_gnn_Wu2, L0_gnn_bu2), axis=-1)
    return x

_drawn_inputs = setup_inputs


def setup_inputs(seed=0):
    import zlib

    import numpy as np

    out = dict(_drawn_inputs(seed))
    spreads = {'L0_gnn_b1': (0.0, 0.1),
     'L0_gnn_b2': (0.0, 0.347),
     'L0_gnn_b3': (0.0, 0.1),
     'L0_gnn_bu1': (0.0, 2.0),
     'L0_gnn_bu2': (0.0, 2.0)}
    factors = {}
    for name, (base, spread) in spreads.items():
        noise = np.random.default_rng([zlib.crc32(name.encode()), seed]).standard_normal(out[name].shape)
        drawn = base * np.exp(spread * noise) if base else spread * noise
        out[name] = jnp.asarray(drawn.astype(out[name].dtype))
    for name, factor in factors.items():
        out[name] = (out[name] * factor).astype(out[name].dtype)
    return out
```

```python
from contextlib import ExitStack

import concourse.bass as bass
from concourse import mybir
import numpy as np

F32 = mybir.dt.float32
BF16 = mybir.dt.bfloat16
I32 = mybir.dt.int32
U16 = mybir.dt.uint16
ALU = mybir.AluOpType
ACT = mybir.ActivationFunctionType
AX = mybir.AxisListType

P = 128
R_CUT = 1.4415
N_RBF = 20
EPS = 1e-5
MAGIC = 1.5 * 2.0 ** 23
TWO_ONES = float(np.array([0x3F803F80], np.uint32).view(np.float32)[0])
TWO_PI = float(np.nextafter(np.float32(2 * np.pi), np.float32(0)))
TJ = 4
GE = TJ * P
PARTS = 6
STACK = (0, 0, 0, 1, 1, 2)
STACK_W = (0, 1, 2, 0, 1, 0)
CHUNKS = 6
PIECES = 6
PB = 3


def build(nc, x, src, dst, ea, ew, W1, b1, W2, b2, W3, b3, U, V, Wu1, bu1, Wu2, bu2, out):
    N, D = x.shape
    E = src.shape[0]
    C = W1.shape[0]
    C3 = 3 * C
    TW = C3 + 2 * C
    NW = -(-N // P)
    NFULL = N // P
    NTAIL = N - NFULL * P
    NT = -(-E // P)
    NGF = E // GE
    ETAIL = E - NGF * GE
    GR = 81
    NPAD = NW * P
    RROWS = CHUNKS * N_RBF
    CH = GR * GE // CHUNKS
    PC = CH // PIECES
    PW = PC // PB
    GW = CHUNKS * CH
    NC1 = N + 1
    CB = NC1 // 3
    W11 = NW + 1
    assert CHUNKS * PIECES * PB * PW == GR * GE and (NT + TJ - 1) * P <= GW and C == P and 3 * CB == NC1
    assert PARTS * N_RBF == RROWS

    node_table = nc.dram_tensor("node_table", (NPAD, TW), F32, kind="Internal").ap()
    rc_rows = nc.dram_tensor("rc_rows", (2, GR * GE), F32, kind="Internal").ap()
    part_rows = nc.dram_tensor("part_rows", (3, RROWS, CH), BF16, kind="Internal").ap()

    with ExitStack() as ctx:
        def sb(name, shape, dt=F32):
            return ctx.enter_context(nc.sbuf_tensor(name, shape, dt))

        def sem(name):
            return ctx.enter_context(nc.semaphore(name))

        psum = ctx.enter_context(nc.psum_tensor("psum", [P, 8, 512], F32))
        bank = [psum[:, i, :] for i in range(8)]

        class Region:

            def __init__(self, ap, width):
                self.ap, self.width, self.at = ap, width, 0

            def cut(self, width, dt=F32, rows=P):
                words = width if dt in (F32, I32) else -(-width // 2)
                a = self.ap[0:rows, self.at:self.at + words]
                self.at += words
                assert self.at <= self.width
                if dt in (BF16, U16):
                    return a.bitcast(dt)[:, 0:width]
                return a if dt == F32 else a.bitcast(dt)

        radial = sb("radial", [P, GW], BF16)
        work = sb("work", [P, NW * D + 2 * TJ * TW])
        side = sb("side", [P, 9424])

        def regions():
            return (Region(radial[:, :].bitcast(F32), GW // 2), Region(work, NW * D + 2 * TJ * TW), Region(side, 9424))

        ident = sb("ident", [P, P])
        node_no = sb("node_no", [P, NPAD + 1])
        ones_row = sb("ones_row", [1, P])
        zeros_bf = sb("zeros_bf", [P, 512], BF16)
        w1 = sb("w1", [P, C])
        w3 = sb("w3", [P, C3])
        u_sb = sb("u_sb", [P, C])
        v_sb = sb("v_sb", [P, C])
        uT = sb("uT", [P, C])
        uv_sb = sb("uv_sb", [P, C])
        wu1 = sb("wu1", [P, 2, C])
        wu2 = sb("wu2", [P, C3])
        b1c = sb("b1c", [P, 1])
        bu1c = sb("bu1c", [P, 1])
        b3r = sb("b3r", [1, C3])
        bu2r = sb("bu2r", [1, C3])
        w2s = sb("w2s", [RROWS + 3, C3], BF16)
        pick = sb("pick", [CHUNKS, 2, N_RBF, CHUNKS])
        half_pi = sb("half_pi", [GR, 1])

        xw = sb("xw", [P, NW, D])
        dst_c = sb("dst_c", [P, GR * TJ])
        src_c = sb("src_c", [P, GR * TJ], I32)
        src_b = sb("src_b", [P, GR * TJ])
        ea_c = sb("ea_c", [P, 3, GR * TJ])
        idx = sb("idx", [P, TJ], I32)
        onehot = sb("onehot", [P, TJ, P])
        onehot_bf = sb("onehot_bf", [P, TJ, P], BF16)
        rng_f = sb("rng_f", [1, 2, W11])
        rng = sb("rng", [1, 2 * W11], I32)

        r_rad, r_work, r_side = regions()
        w2f = r_rad.cut(C3, rows=N_RBF)
        b2f = r_rad.cut(C3, rows=1)
        w2p = r_rad.cut(3 * C3, BF16, rows=N_RBF).rearrange("p (k f) -> p k f", k=3)
        b2p = r_rad.cut(3 * C3, BF16, rows=1).rearrange("p (k f) -> p k f", k=3)
        node_no_i = r_rad.cut(NPAD + 1, I32)
        pick_i = r_rad.cut(2 * RROWS, I32, rows=CHUNKS).rearrange("p (k n c) -> p k n c", k=2, n=N_RBF)
        src_i = r_work.cut(GE, I32, rows=GR)
        dst_i = r_work.cut(GE, I32, rows=GR)
        dst_hi_i = r_work.cut(GE, I32, rows=GR)
        ea_r = r_work.cut(3 * GE, rows=GR)
        r_r = r_work.cut(GE, rows=GR)
        src_f = r_work.cut(GE, rows=GR)
        dst_f = r_work.cut(GE, rows=GR)
        coef = r_work.cut(GE, rows=GR)
        tmp_a = r_work.cut(GE, rows=GR)
        tmp_b = r_work.cut(GE, rows=GR)
        sT = r_work.cut(NPAD)
        hT = r_work.cut(NPAD)
        table_out = r_work.cut(2 * TW).rearrange("p (b f) -> p b f", b=2)
        turn = r_side.cut(PC, rows=RROWS).rearrange("p (b f) -> p b f", b=PB)
        wave = r_side.cut(2 * PC, rows=RROWS).rearrange("p (d f) -> p d f", d=2)
        part = r_side.cut(6 * PC, BF16, rows=RROWS).rearrange("p (d k f) -> p d k f", d=2, k=3)
        rc_piece = r_side.cut(2 * PC, rows=CHUNKS).rearrange("p (k f) -> p k f", k=2)
        first_filter = onehot[:, 0:2, :]
        tile_no_i = r_work.cut(TJ, I32, rows=GR)
        tile_no = r_work.cut(TJ, rows=GR)
        win_lo_i = r_work.cut(W11, I32, rows=GR)
        win_lo = r_work.cut(W11, rows=GR)
        least = r_work.cut(TJ, rows=GR)
        most = r_work.cut(TJ, rows=GR)
        to_last = r_work.cut(TJ, rows=GR)
        past = r_work.cut(TJ, rows=GR)
        in_span = r_work.cut(W11, rows=GR)
        span = r_work.cut(TJ * 2 * W11, rows=GR).rearrange("p (j k w) -> p j k w", j=TJ, k=2)
        span_t = r_work.cut(1, rows=TJ * 2 * W11)

        r_rad, r_work, r_side = regions()
        x1 = r_work.cut(NW * D).rearrange("p (w f) -> p w f", w=NW)
        rows_in = r_work.cut(TJ * TW).rearrange("p (j f) -> p j f", j=TJ)
        msg = r_work.cut(TJ * TW).rearrange("p (j f) -> p j f", j=TJ)
        cumul = r_side.cut(NW * (NC1 + 1), U16).rearrange("p (w f) -> p w f", w=NW)
        sign = r_side.cut(2 * (NC1 + 1), BF16).rearrange("p (b f) -> p b f", b=2)
        half_deg = r_side.cut(1)

        r_rad, r_work, r_side = regions()
        countsT = r_rad.cut(NW * NPAD).rearrange("p (s d) -> p s d", s=NW)
        vu = r_rad.cut(NW * C3).rearrange("p (w f) -> p w f", w=NW)
        vv = r_rad.cut(NW * C3).rearrange("p (w f) -> p w f", w=NW)
        r_work.cut(NW * D)
        x1T = r_work.cut(2 * D).rearrange("p (b f) -> p b f", b=2)
        sT1 = r_work.cut(NPAD)
        nrm = r_work.cut(NPAD).rearrange("p (w f) -> p w f", w=NW)
        nT = r_work.cut(NPAD)
        r_side.cut(NW * (NC1 + 1), U16)
        h1T = r_side.cut(NPAD)
        counts_f = r_side.cut(NPAD)
        sq = r_side.cut(C3)
        stat = r_side.cut(NW * 12).rearrange("p (w f) -> p w f", w=NW)
        ssq = r_work.cut(2 * C).rearrange("p (b f) -> p b f", b=2)
        prod, dot = sq, ssq[:, 0, :]
        y = x1T
        hh = x1T[:, :, 0:C3]

        names = """ld_x ld_r ld_edges ld_weights pads_set pool_const picks_made dve_const half_pi_set dve_step cos_in
        cos_done rc_made rc_stored rc_spread turn_made sin_done wave_scaled hi_made wave_less_hi mid_made lo_made
        parts_moved w2_split w2_moved edges_float edges_turned edges_taken span_made span_turned span_max span_row
        ranges_set s_turned s_taken z_made sig_made h_made filter_made filter_taken table_vec_made table_rest_made
        uv_turned uv_taken uv_made uv_set window_summed banks_free half_made
        node_added x1T_turned x1T_taken v_made v_taken v_squared norm_sq norm_made norm_turned norm_taken s1_taken
        z1_made sig1_made h1_made gate_made gate_taken update_made counts_float counts_turned counts_taken
        window_done res_made ln_stats ln_mean var_made std_made ln_scale y_made y_stored turn_read x_residual""".split()
        S = {n: sem(n) for n in names}
        rc_loaded = sem("rc_loaded")
        parts_stored = [sem(f"parts_stored{b}") for b in range(2)]
        table_stored = [sem(f"table_stored{b}") for b in range(2)]
        gathered = [sem(f"gathered{j}") for j in range(TJ)]
        indices_set = [sem(f"indices_set{q}") for q in range(2)]
        rows_used = [sem(f"rows_used{q}") for q in range(2)]
        basis_made = [sem(f"basis_made{q}") for q in range(2)]
        hot_made = [sem(f"hot_made{j}") for j in range(TJ)]
        msg_made = [sem(f"msg_made{j}") for j in range(TJ)]
        summed = [sem(f"summed{j}") for j in range(TJ)]
        sign_made = [sem(f"sign_made{b}") for b in range(2)]
        sign_used = [sem(f"sign_used{b}") for b in range(2)]
        THIRDS = ((0, 512), (512, 1024), (1024, NPAD))

        EARLY = 3

        def out_bank(w):
            return 5 + w if w < EARLY else (w - EARLY) % 4

        def through(n, b):
            return (n + 1 - b) // 2

        def window_range(eng, w):
            first = eng.value_load(rng[0:1, bass.ds(w, 1)], min_val=0, max_val=NT - 1)
            end = eng.value_load(rng[0:1, bass.ds(w + W11, 1)], min_val=1, max_val=NT)
            return first, end

        block = ctx.enter_context(nc.Block())

        @block.sync
        def _(sp):
            def load_rows(a, b_, width, done):
                sp.dma_start(a[0:NGF, :], b_[0:NGF * GE * width].rearrange("(g f) -> g f", f=GE * width)).then_inc(done, 16)
                sp.dma_start(a[NGF:NGF + 1, 0:ETAIL * width],
                             b_[NGF * GE * width:E * width].rearrange("(g f) -> g f", g=1)).then_inc(done, 16)

            sp.dma_start(w2f, W2).then_inc(S["ld_weights"], 16)
            sp.dma_start(b2f, b2.rearrange("(a f) -> a f", a=1)).then_inc(S["ld_weights"], 16)
            sp.wait_ge(S["pads_set"], 1)
            load_rows(r_r, ew, 1, S["ld_r"])
            sp.wait_ge(S["pads_set"], 6)
            for a, b_, width in ((dst_i, dst, 1), (dst_hi_i, dst, 1), (src_i, src, 1), (ea_r, ea.rearrange("e k -> (e k)"), 3)):
                load_rows(a, b_, width, S["ld_edges"])
            sp.dma_start(xw[:, 0:NFULL, :], x[0:NFULL * P, :].rearrange("(w p) f -> p w f", p=P)).then_inc(S["ld_x"], 16)
            sp.dma_start(xw[0:NTAIL, NFULL, :], x[NFULL * P:N, :]).then_inc(S["ld_x"], 16)
            for a, b_ in ((w1[:, :], W1), (w3[:, :], W3), (b1c[:, :], b1.rearrange("(p a) -> p a", a=1)),
                          (b3r[:, :], b3.rearrange("(a f) -> a f", a=1)), (u_sb[:, :], U), (v_sb[:, :], V),
                          (wu1[:, :, :], Wu1.rearrange("(k p) f -> p k f", p=P)),
                          (bu1c[:, :], bu1.rearrange("(p a) -> p a", a=1)), (wu2[:, :], Wu2),
                          (bu2r[:, :], bu2.rearrange("(a f) -> a f", a=1))):
                sp.dma_start(a, b_).then_inc(S["ld_weights"], 16)
            sp.wait_ge(S["w2_split"], 2)
            for q, k in enumerate(STACK_W):
                sp.dma_start(w2s[q * N_RBF:(q + 1) * N_RBF, :], w2p[:, k, :]).then_inc(S["w2_moved"], 16)
            for k in range(3):
                sp.dma_start(w2s[RROWS + k:RROWS + k + 1, :], b2p[:, k, :]).then_inc(S["w2_moved"], 16)
            sp.wait_ge(S["rc_made"], 1)
            sp.dma_start(rc_rows[0].rearrange("(g f) -> g f", f=GE), r_r).then_inc(S["rc_stored"], 16)
            sp.dma_start(rc_rows[1].rearrange("(g f) -> g f", f=GE), coef).then_inc(S["rc_stored"], 16)
            sp.wait_ge(S["rc_stored"], 32)

            def load_piece(i):
                if i:
                    sp.wait_ge(S["rc_spread"], 2 * i)
                for k in range(2):
                    sp.dma_start(rc_piece[:, k, :], rc_rows[k, 0:GW].rearrange("(c f) -> c f", c=CHUNKS)[:, i * PC:(i + 1) * PC]
                                 ).then_inc(rc_loaded, 16)

            def store_table(w):
                sp.wait_ge(S["table_vec_made"], w + 1)
                sp.wait_ge(S["table_rest_made"], w + 1)
                sp.dma_start(node_table[w * P:(w + 1) * P, :], table_out[:, w % 2, :]).then_inc(table_stored[w % 2], 16)

            load_piece(0)
            for i in range(PIECES):
                if i + 1 < PIECES:
                    load_piece(i + 1)
                for w in (2 * i, 2 * i + 1):
                    if w < NW:
                        store_table(w)
                o = i * PC
                sp.wait_ge(S["lo_made"], i + 1)
                sp.dma_start(part_rows[:, :, o:o + PC].rearrange("k p f -> p k f"), part[:, i % 2, :, :]
                             ).then_inc(parts_stored[i % 2], 16)
                sp.wait_ge(parts_stored[i % 2], 16 * (i // 2 + 1))
                sp.wait_ge(S["pads_set"], 7)
                for q, k in enumerate(STACK):
                    sp.dma_start(radial[q * N_RBF:(q + 1) * N_RBF, :].rearrange("p (c f) -> p c f", c=CHUNKS)[:, :, o:o + PC],
                                 part_rows[k].rearrange("(n c) f -> n c f", c=CHUNKS)[:, :, o:o + PC]
                                 ).then_inc(S["parts_moved"], 16)
            for w in range(NW):
                n = P if w < NFULL else NTAIL
                sp.wait_ge(S["y_made"], w + 1)
                sp.dma_start(out[w * P:w * P + n, :], xw[0:n, w, :]).then_inc(S["y_stored"], 16)
            sp.wait_ge(S["y_stored"], 16 * NW)

        @block.gpsimd
        def _(pool):
            g = nc.gpsimd
            g.memset(r_r, 1.0).then_inc(S["pads_set"], 1)
            g.memset(dst_i, -1).then_inc(S["pads_set"], 1)
            g.memset(dst_hi_i, 2 * NPAD).then_inc(S["pads_set"], 1)
            g.memset(src_i, 0).then_inc(S["pads_set"], 1)
            g.memset(ea_r, 0.0).then_inc(S["pads_set"], 1)
            g.memset(xw[:, NFULL, :], 0.0).then_inc(S["pads_set"], 1)
            g.iota(pick_i[:, 0], pattern=[[1, N_RBF], [0, CHUNKS]], base=1, channel_multiplier=0).then_inc(S["pool_const"], 1)
            g.iota(pick_i[:, 1], pattern=[[0, N_RBF], [1, CHUNKS]], base=0, channel_multiplier=-1).then_inc(S["pool_const"], 1)
            g.memset(ident[:, :], 0.0).then_inc(S["pool_const"], 1)
            pool.wait_ge(S["pool_const"], 3)
            g.affine_select(out=ident[:, :], in_=ident[:, :], compare_op=ALU.not_equal, fill=1.0, base=0,
                            pattern=[[-1, P]], channel_multiplier=1).then_inc(S["pool_const"], 1)
            g.iota(tile_no_i[:, :], pattern=[[1, TJ]], base=0, channel_multiplier=TJ).then_inc(S["pool_const"], 1)
            g.iota(win_lo_i[:, :], pattern=[[P, W11]], base=0, channel_multiplier=0).then_inc(S["pool_const"], 1)
            g.iota(node_no_i, pattern=[[1, NPAD + 1]], base=-1, channel_multiplier=0).then_inc(S["pool_const"], 1)
            pool.wait_ge(S["dve_const"], 3)
            pool.wait_ge(S["picks_made"], 2)
            pool.wait_ge(S["w2_moved"], 16 * (PARTS + 3))
            g.memset(radial[96:P, :].bitcast(F32), TWO_ONES).then_inc(S["pads_set"], 1)
            pool.wait_ge(S["pads_set"], 7)
            for i in range(PIECES):
                b = i % 2
                pool.wait_ge(S["hi_made"], i + 1)
                g.tensor_tensor(wave[:, b, :], wave[:, b, :], part[:, b, 0, :], ALU.subtract).then_inc(S["wave_less_hi"], 1)
                pool.wait_ge(S["mid_made"], i + 1)
                g.tensor_tensor(part[:, b, 2, :], wave[:, b, :], part[:, b, 1, :], ALU.subtract).then_inc(S["lo_made"], 1)

            turns = pool.alloc_register("group_turn")
            pool.reg_mov(turns, 1)
            odd_turns = pool.alloc_register("group_turn_twice_less_1")
            pool.reg_mov(odd_turns, 1)
            pool.wait_ge(S["ranges_set"], 1)
            pool.wait_ge(S["edges_taken"], 6)
            pool.wait_ge(S["lo_made"], PIECES)
            for b in range(2):
                pool.wait_ge(table_stored[b], 16 * through(NW, b))

            def gathers(w):
                first, end = window_range(pool, w)
                with pool.Fori(first, end, TJ) as t:
                    n1 = pool.snap(turns)
                    u = pool.snap(odd_turns)
                    at = pool.snap(t, min_val=0, max_val=NT - 1)
                    for q in range(2):
                        pair = slice(2 * q, 2 * q + 2)
                        pool.wait_ge(S["ranges_set"], 1)
                        pool.wait_ge(rows_used[q], u)
                        g.tensor_copy(idx[:, pair], src_c[:, bass.ds(at + 2 * q, 2)]).then_inc(indices_set[q], 1)
                        for j in (2 * q, 2 * q + 1):
                            pool.wait_ge(S["ranges_set"], 1)
                            if j == 2 * q:
                                pool.wait_ge(indices_set[q], n1)
                            g.indirect_dma_start(
                                out=rows_in[:, j, :], out_offset=None, in_=node_table,
                                in_offset=bass.IndirectOffsetOnAxis(ap=idx[:, j:j + 1], axis=0)).then_inc(gathered[j], 16)
                    pool.reg_add(turns, turns, 1)
                    pool.reg_add(odd_turns, odd_turns, 2)

            with pool.Fori(0, NW) as w:
                gathers(w)
            pool.wait_ge(S["banks_free"], 2 * NW + 2)
            g.memset(counts_f[:, N:NPAD], 0.0).then_inc(S["counts_float"], 1)
            for w in range(NW):
                g.tensor_tensor(x1[:, w, :], x1[:, w, :], xw[:, w, :], ALU.add).then_inc(S["node_added"], 1)
                pool.wait_ge(S["node_added"], w + 1)
                g.tensor_tensor(xw[:, w, :], xw[:, w, :], x1[:, w, :], ALU.add).then_inc(S["x_residual"], 1)

        @block.scalar
        def _(act):
            a = nc.scalar
            act.sem_inc(S["banks_free"], 2)
            act.wait_ge(S["cos_in"], 1)
            act.wait_ge(S["half_pi_set"], 1)
            a.activation(tmp_b, tmp_a, ACT.Sin, bias=half_pi[:, :], scale=-float(np.pi / R_CUT)).then_inc(S["cos_done"], 1)
            for c, (lo, hi) in enumerate(THIRDS):
                act.wait_ge(S["z_made"], c + 1)
                a.activation(hT[:, lo:hi], bank[5 + c][:, 0:hi - lo], ACT.Sigmoid, bias=b1c[:, :]).then_inc(S["sig_made"], 1)

            def take_filter(w):
                b = w % 2
                act.wait_ge(S["filter_made"], w + 1)
                if w >= 2:
                    act.wait_ge(table_stored[b], 16 * (w // 2))
                    act.wait_ge(S["table_vec_made"], w - 1)
                a.copy(first_filter[:, b, :], bank[6 + b][:, 0:C]).then_inc(S["filter_taken"], 1)
                a.copy(table_out[:, b, C3:TW], bank[6 + b][:, C:C3]).then_inc(S["table_rest_made"], 1)

            def middle(i):
                act.wait_ge(S["wave_less_hi"], i + 1)
                a.copy(part[:, i % 2, 1, :], wave[:, i % 2, :]).then_inc(S["mid_made"], 1)

            for i in range(PIECES):
                b = i % 2
                act.wait_ge(S["turn_made"], i + 1)
                if i >= 2:
                    act.wait_ge(S["lo_made"], i - 1)
                a.activation(wave[:, b, :], turn[:, :, :].rearrange("p b f -> p (b f)"), ACT.Sin, scale=TWO_PI
                             ).then_inc(S["sin_done"], 1)
                if i:
                    middle(i - 1)
                act.wait_ge(S["wave_scaled"], i + 1)
                if i >= 2:
                    act.wait_ge(parts_stored[b], 16 * (i // 2))
                a.copy(part[:, b, 0, :], wave[:, b, :]).then_inc(S["hi_made"], 1)
                for w in (2 * i, 2 * i + 1):
                    if w < NW:
                        take_filter(w)
            middle(PIECES - 1)

            turns = act.alloc_register("signed_group_turn")
            act.reg_mov(turns, 1)
            act.wait_ge(S["ranges_set"], 1)
            act.wait_ge(S["edges_taken"], 6)
            act.wait_ge(S["lo_made"], PIECES)
            act.wait_ge(S["rc_spread"], 2 * PIECES)
            for b in range(2):
                act.wait_ge(parts_stored[b], 16 * through(PIECES, b))
            with act.Fori(0, NW) as w:
                first, end = window_range(act, w)
                with act.Fori(first, end, TJ) as t:
                    n1 = act.snap(turns)
                    for j in range(TJ):
                        b = j % 2
                        act.wait_ge(sign_used[b], 2 * n1 - 1 + j // 2)
                        a.activation(sign[:, b, 0:NC1], node_no[:, 0:NC1], ACT.Sign,
                                     bias=src_b[:, bass.ds(t + j, 1)]).then_inc(sign_made[b], 1)
                    act.reg_add(turns, turns, 1)
                act.wait_ge(S["window_summed"], w + 1)
                a.copy(x1[:, bass.ds(w, 1), :], bank[4].unsqueeze(1)).then_inc(S["banks_free"], 1)
                a.mul(half_deg, psum[:, 5, 0:1], -0.5).then_inc(S["half_made"], 1)
                act.wait_ge(S["half_made"], w + 1)
                a.activation(cumul[:, bass.ds(w, 1), 0:NC1].rearrange("p a (b f) -> p (a b) f", b=3), psum[:, 5:8, 0:CB], ACT.Identity,
                             bias=half_deg, scale=0.5).then_inc(S["banks_free"], 1)

            for w in range(NW):
                b = w % 2
                act.wait_ge(S["x1T_turned"], w + 1)
                if w >= 2:
                    act.wait_ge(S["v_made"], w - 1)
                    act.wait_ge(S["s1_taken"], w - 1)
                a.copy(x1T[:, b, :], bank[b]).then_inc(S["x1T_taken"], 1)
                act.wait_ge(S["v_made"], w + 1)
                a.copy(vu[:, w, :], bank[2 + b][:, 0:C3]).then_inc(S["v_taken"], 1)
                a.copy(vv[:, w, :], bank[4 + b][:, 0:C3]).then_inc(S["v_taken"], 1)
                if w:
                    act.wait_ge(S["norm_sq"], w)
                a.activation(sq[:, :], bank[4 + b][:, 0:C3], ACT.Square).then_inc(S["v_squared"], 1)
                if w:
                    act.wait_ge(S["norm_sq"], w)
                    a.activation(nrm[:, w - 1, :], ssq[:, (w - 1) % 2, :], ACT.Sqrt).then_inc(S["norm_made"], 1)
            act.wait_ge(S["norm_sq"], NW)
            a.activation(nrm[:, NW - 1, :], ssq[:, (NW - 1) % 2, :], ACT.Sqrt).then_inc(S["norm_made"], 1)
            for c, (lo, hi) in enumerate(THIRDS):
                act.wait_ge(S["z1_made"], c + 1)
                a.activation(h1T[:, lo:hi], bank[c][:, 0:hi - lo], ACT.Sigmoid, bias=bu1c[:, :]).then_inc(S["sig1_made"], 1)
            for w in range(NW):
                act.wait_ge(S["gate_made"], w + 1)
                if w >= 2:
                    act.wait_ge(S["update_made"], 2 * (w - 1))
                a.copy(hh[:, w % 2, :], bank[3 + w % 2][:, 0:C3]).then_inc(S["gate_taken"], 1)
            for w in range(NW):
                act.wait_ge(S["var_made"], w + 1)
                a.activation(stat[:, w, 9:10], stat[:, w, 8:9], ACT.Sqrt).then_inc(S["std_made"], 1)

        @block.vector
        def _(dve):
            v = nc.vector
            steps = [0]

            def then(ins):
                steps[0] += 1
                ins.then_inc(S["dve_step"], 1)
                dve.wait_ge(S["dve_step"], steps[0])

            for q in range(2):
                dve.sem_inc(rows_used[q], 1)
            v.memset(half_pi[:, :], float(np.pi / 2)).then_inc(S["half_pi_set"], 1)
            v.memset(ones_row[:, :], 1.0).then_inc(S["dve_const"], 1)
            v.memset(zeros_bf[:, :], 0.0).then_inc(S["dve_const"], 1)
            dve.wait_ge(S["ld_r"], 32)
            v.tensor_scalar(tmp_a, r_r, R_CUT, None, ALU.min).then_inc(S["cos_in"], 1)
            then(v.reciprocal(coef, r_r))
            dve.wait_ge(S["cos_done"], 1)
            k = 0.5 * float(np.sqrt(np.float32(2.0 / R_CUT)))
            then(v.tensor_scalar(tmp_b, tmp_b, 1.0, k, ALU.add, ALU.mult))
            then(v.scalar_tensor_tensor(out=tmp_b, in0=r_r, scalar=R_CUT, in1=tmp_b, op0=ALU.is_lt, op1=ALU.mult))
            v.tensor_tensor(coef, tmp_b, coef, ALU.mult).then_inc(S["rc_made"], 1)
            dve.wait_ge(S["ld_weights"], 16 * 12)
            for full, parts in ((w2f, w2p), (b2f, b2p)):
                then(v.tensor_copy(parts[:, 0, :], full))
                then(v.tensor_tensor(full, full, parts[:, 0, :], ALU.subtract))
                then(v.tensor_copy(parts[:, 1, :], full))
                v.tensor_tensor(parts[:, 2, :], full, parts[:, 1, :], ALU.subtract).then_inc(S["w2_split"], 1)
            dve.wait_ge(S["pool_const"], 7)
            v.tensor_scalar(pick[:, 1], pick_i[:, 1], 0.0, None, ALU.is_equal).then_inc(S["picks_made"], 1)
            dve.wait_ge(S["picks_made"], 1)
            v.scalar_tensor_tensor(out=pick[:, 0], in0=pick_i[:, 0], scalar=1.0 / (2 * R_CUT), in1=pick[:, 1],
                                   op0=ALU.mult, op1=ALU.mult).then_inc(S["picks_made"], 1)
            v.tensor_copy(node_no[:, :], node_no_i).then_inc(S["dve_const"], 1)
            dve.wait_ge(S["ld_edges"], 16 * 8)
            v.tensor_copy(src_f, src_i).then_inc(S["edges_float"], 1)
            dve.wait_ge(S["rc_made"], 1)
            v.tensor_copy(dst_f, dst_i).then_inc(S["edges_float"], 1)
            dve.wait_ge(S["edges_float"], 2)
            then(v.tensor_copy(tmp_a, dst_hi_i))
            then(v.tensor_copy(tile_no[:, :], tile_no_i[:, :]))
            then(v.tensor_copy(win_lo[:, :], win_lo_i[:, :]))
            then(v.tensor_reduce(most[:, :], dst_f.rearrange("g (j f) -> g j f", j=TJ), AX.X, ALU.max))
            then(v.tensor_reduce(least[:, :], tmp_a.rearrange("g (j f) -> g j f", j=TJ), AX.X, ALU.min))
            then(v.tensor_scalar(to_last[:, :], tile_no[:, :], -1.0, float(NT), ALU.mult, ALU.add))
            then(v.tensor_scalar(past[:, :], tile_no[:, :], 1.0, None, ALU.add))
            for j in range(TJ):
                then(v.tensor_scalar(in_span[:, :], win_lo[:, :], float(P - 1), least[:, j:j + 1], ALU.add, ALU.is_ge))
                then(v.scalar_tensor_tensor(out=in_span[:, :], in0=win_lo[:, :], scalar=most[:, j:j + 1], in1=in_span[:, :],
                                            op0=ALU.is_le, op1=ALU.mult))
                v.tensor_scalar(span[:, j, 0, :], in_span[:, :], to_last[:, j:j + 1], -float(NT), ALU.mult,
                                ALU.add).then_inc(S["span_made"], 1)
                v.tensor_scalar(span[:, j, 1, :], in_span[:, :], past[:, j:j + 1], None, ALU.mult).then_inc(S["span_made"], 1)
                dve.wait_ge(S["span_made"], 2 * j + 2)
            dve.wait_ge(S["span_turned"], 1)
            v.tensor_reduce(span_t[:, :], bank[5][0:TJ * 2 * W11, 0:GR], AX.X, ALU.max).then_inc(S["span_max"], 1)
            dve.wait_ge(S["span_row"], 1)
            then(v.tensor_reduce(rng_f[:, :, :].rearrange("p a b -> p (a b)"),
                                 bank[5][0:1, 128:128 + TJ * 2 * W11].rearrange("p (j c) -> p c j", j=TJ), AX.X, ALU.max))
            lo_f, end_f = rng_f[0:1, 0, :], rng_f[0:1, 1, :]
            then(v.tensor_scalar(lo_f, lo_f, -1.0, float(NT - 1), ALU.mult, ALU.min))
            then(v.scalar_tensor_tensor(out=end_f, in0=lo_f, scalar=1.0, in1=end_f, op0=ALU.add, op1=ALU.max))
            v.tensor_copy(rng[:, :], rng_f[:, :, :].rearrange("p a b -> p (a b)")).then_inc(S["ranges_set"], 1)
            dve.wait_ge(S["edges_turned"], 5)

            def columns(ap):
                return ap.rearrange("p (g j) -> p j g", j=TJ)

            def turned(i):
                return bank[i][:, 0:TJ * GR].rearrange("p (j g) -> p j g", j=TJ)

            v.tensor_copy(columns(dst_c[:, :]), turned(0)).then_inc(S["edges_taken"], 1)
            v.tensor_copy(columns(src_c[:, :]), turned(1)).then_inc(S["edges_taken"], 1)
            v.tensor_scalar(columns(src_b[:, :]), turned(1), -1.0, 0.5, ALU.mult, ALU.add).then_inc(S["edges_taken"], 1)
            for c in range(3):
                v.tensor_copy(columns(ea_c[:, c]), turned(2 + c)).then_inc(S["edges_taken"], 1)
            for c, (lo, hi) in enumerate(THIRDS):
                dve.wait_ge(S["s_turned"], c + 1)
                v.tensor_copy(sT[:, lo:hi], bank[5 + c][:, 0:hi - lo]).then_inc(S["s_taken"], 1)
            for c, (lo, hi) in enumerate(THIRDS):
                dve.wait_ge(S["sig_made"], c + 1)
                v.scalar_tensor_tensor(out=hT[:, lo:hi], in0=bank[5 + c][:, 0:hi - lo], scalar=b1c[:, :], in1=hT[:, lo:hi],
                                       op0=ALU.add, op1=ALU.mult).then_inc(S["h_made"], 1)
            dve.wait_ge(S["uv_turned"], 1)
            v.tensor_copy(uT[:, :], bank[6][:, 0:C]).then_inc(S["uv_taken"], 1)
            dve.wait_ge(S["uv_made"], 1)
            v.tensor_copy(uv_sb[:, :], bank[7][:, 0:C]).then_inc(S["uv_set"], 1)
            for i in range(PIECES):
                turns_x, coef_x = psum[0:RROWS, 0:PB, 0:PW], psum[0:RROWS, PB:2 * PB, 0:PW]
                dve.wait_ge(S["rc_spread"], 2 * i + 1)
                if i:
                    dve.wait_ge(S["sin_done"], i)
                then(v.tensor_scalar(turn, turns_x, MAGIC, MAGIC, ALU.add, ALU.subtract))
                v.tensor_tensor(turn, turns_x, turn, ALU.subtract).then_inc(S["turn_made"], 1)
                dve.wait_ge(S["sin_done"], i + 1)
                dve.wait_ge(S["rc_spread"], 2 * i + 2)
                wv = wave[:, i % 2, :].rearrange("p (b f) -> p b f", b=PB)
                v.tensor_tensor(wv, wv, coef_x, ALU.mult).then_inc(S["wave_scaled"], 1)
                for w in (2 * i, 2 * i + 1):
                    if w < NW:
                        dve.wait_ge(S["filter_taken"], w + 1)
                        if w >= 2:
                            dve.wait_ge(table_stored[w % 2], 16 * (w // 2))
                        v.tensor_tensor(table_out[:, w % 2, 0:C3].rearrange("p (c k) -> p c k", k=3),
                                        xw[:, w, 0:C3].rearrange("p (c k) -> p c k", k=3),
                                        first_filter[:, w % 2, :].unsqueeze(2).to_broadcast((P, C, 3)),
                                        ALU.mult).then_inc(S["table_vec_made"], 1)

            turns = dve.alloc_register("message_group_turn")
            dve.reg_mov(turns, 1)
            with dve.Fori(0, NW) as w:
                first, end = window_range(dve, w)
                with dve.Fori(first, end, TJ) as t:
                    n1 = dve.snap(turns)
                    for q in range(2):
                        pair = slice(2 * q, 2 * q + 2)
                        vec = msg[:, pair, 0:C3].rearrange("p j (c k) -> p j c k", k=3)
                        for j in (2 * q, 2 * q + 1):
                            dve.wait_ge(summed[j], n1)
                            nodes = node_no[:, bass.ds(w * P + 1, P)]
                            v.tensor_scalar(onehot[:, j, :], nodes, dst_c[:, bass.ds(t + j, 1)], None,
                                            ALU.is_equal).then_inc(msg_made[j], 1)
                            v.tensor_scalar(onehot_bf[:, j, :], nodes, dst_c[:, bass.ds(t + j, 1)], None,
                                            ALU.is_equal).then_inc(hot_made[j], 1)
                        dve.wait_ge(gathered[2 * q], n1 * 16)
                        dve.wait_ge(gathered[2 * q + 1], n1 * 16)
                        dve.wait_ge(basis_made[q], n1)
                        v.tensor_tensor(msg[:, pair, C3:TW], rows_in[:, pair, C3:TW], psum[:, pair, C:C3],
                                        ALU.mult).then_inc(rows_used[q], 1)
                        v.tensor_tensor(vec, rows_in[:, pair, 0:C3].rearrange("p j (c k) -> p j c k", k=3),
                                        psum[:, pair, 0:C].unsqueeze(3).to_broadcast((P, 2, C, 3)),
                                        ALU.mult).then_inc(rows_used[q], 1)
                        dve.wait_ge(rows_used[q], n1 * 2 + 1)
                        for j in (2 * q, 2 * q + 1):
                            for c in range(3):
                                comp = msg[:, j, 0:C3].rearrange("p (c k) -> p c k", k=3)[:, :, c]
                                v.scalar_tensor_tensor(out=comp, in0=msg[:, j, D:TW], scalar=ea_c[:, c, bass.ds(t + j, 1)],
                                                       in1=comp, op0=ALU.mult, op1=ALU.add).then_inc(msg_made[j], 1)
                    dve.reg_add(turns, turns, 1)

            def take_counts(w):
                for c in range(3):
                    k0, k1 = 4 * c, min(NW, 4 * c + 4)
                    m = 3 * w + c
                    dve.wait_ge(S["counts_turned"], m + 1)
                    v.tensor_copy(countsT[:, k0:k1, w * P:(w + 1) * P],
                                  bank[6 + m % 2][:, 0:(k1 - k0) * P].rearrange("p (k f) -> p k f", f=P)
                                  ).then_inc(S["counts_taken"], 1)

            def difference(w):
                v.tensor_tensor(counts_f[:, 0:N], cumul[:, w, 1:NC1], cumul[:, w, 0:N], ALU.subtract).then_inc(S["counts_float"], 1)

            dve.wait_ge(S["banks_free"], 2 * NW + 2)
            difference(0)
            for w in range(NW):
                b = w % 2
                dve.wait_ge(S["x1T_taken"], w + 1)
                v.tensor_copy(sT1[:, w * P:(w + 1) * P], x1T[:, b, C3:D]).then_inc(S["s1_taken"], 1)
                take_counts(w)
                if w + 1 < NW:
                    difference(w + 1)
                dve.wait_ge(S["v_squared"], w + 1)
                if w >= 2:
                    dve.wait_ge(S["norm_made"], w - 1)
                then(v.tensor_reduce(ssq[:, b, :], sq[:, :].rearrange("p (c k) -> p c k", k=3), AX.X, ALU.add))
                v.tensor_scalar(ssq[:, b, :], ssq[:, b, :], 2.0 ** -115, None, ALU.max).then_inc(S["norm_sq"], 1)
            for c, (lo, hi) in enumerate(THIRDS):
                dve.wait_ge(S["norm_turned"], min(NW, (c + 1) * 4))
                v.tensor_copy(nT[:, lo:hi], bank[5 + c][:, 0:hi - lo]).then_inc(S["norm_taken"], 1)
            for c, (lo, hi) in enumerate(THIRDS):
                dve.wait_ge(S["sig1_made"], c + 1)
                v.scalar_tensor_tensor(out=h1T[:, lo:hi], in0=bank[c][:, 0:hi - lo], scalar=bu1c[:, :], in1=h1T[:, lo:hi],
                                       op0=ALU.add, op1=ALU.mult).then_inc(S["h1_made"], 1)
            for w in range(NW):
                b = w % 2
                dve.wait_ge(S["gate_taken"], w + 1)
                dve.wait_ge(S["x_residual"], w + 1)
                vec = x1[:, w, 0:C3].rearrange("p (c k) -> p c k", k=3)
                v.tensor_tensor(vec, vu[:, w, :].rearrange("p (c k) -> p c k", k=3),
                                hh[:, b, 0:C].unsqueeze(2).to_broadcast((P, C, 3)), ALU.mult).then_inc(S["update_made"], 1)
                dve.wait_ge(S["update_made"], 2 * w + 1)
                then(v.tensor_tensor(prod[:, :], x1[:, w, 0:C3], vv[:, w, :], ALU.mult))
                then(v.tensor_reduce(dot, prod[:, :].rearrange("p (c k) -> p c k", k=3), AX.X, ALU.add))
                v.tensor_tensor(x1[:, w, C3:D], dot, hh[:, b, 2 * C:C3], ALU.add).then_inc(S["update_made"], 1)

            for w in range(NW):
                res, st = y[:, w % 2, :], stat[:, w, :]
                dve.wait_ge(S["window_done"], w + 1)
                v.tensor_tensor(res, xw[:, w, :], bank[out_bank(w)], ALU.add).then_inc(S["res_made"], 1)
                dve.wait_ge(S["res_made"], w + 1)
                v.bn_stats(st[:, 0:6], res).then_inc(S["ln_stats"], 1)
                dve.wait_ge(S["ln_stats"], w + 1)
                v.bn_aggr(st[:, 6:8], st[:, 0:6]).then_inc(S["ln_mean"], 1)
                dve.wait_ge(S["ln_mean"], w + 1)
                v.tensor_scalar(st[:, 8:9], st[:, 7:8], EPS, None, ALU.add).then_inc(S["var_made"], 1)
                dve.wait_ge(S["std_made"], w + 1)
                v.reciprocal(st[:, 10:11], st[:, 9:10]).then_inc(S["ln_scale"], 1)
                dve.wait_ge(S["ln_scale"], w + 1)
                v.tensor_scalar(xw[:, w, :], res, st[:, 6:7], st[:, 10:11], ALU.subtract, ALU.mult).then_inc(S["y_made"], 1)

        @block.tensor
        def _(pe):
            mm = nc.tensor.matmul
            turn_ = nc.tensor.transpose
            for j in range(TJ):
                pe.sem_inc(summed[j], 1)
            for b in range(2):
                pe.sem_inc(sign_used[b], 1)
            pe.wait_ge(S["pool_const"], 4)
            pe.wait_ge(S["edges_float"], 2)
            ea_k = ea_r.rearrange("g (e k) -> g e k", k=3)
            for i, a in enumerate((dst_f, src_f, ea_k[:, :, 0], ea_k[:, :, 1], ea_k[:, :, 2])):
                for j in range(TJ):
                    last = turn_(bank[i][:, j * GR:(j + 1) * GR], a[:, j * P:(j + 1) * P], ident[0:GR, 0:GR])
                last.then_inc(S["edges_turned"], 1)
            pe.wait_ge(S["span_made"], 2 * TJ)
            turn_(bank[5][0:TJ * 2 * W11, 0:GR], span[:, :, :, :].rearrange("p a b c -> p (a b c)"),
                  ident[0:GR, 0:GR]).then_inc(S["span_turned"], 1)
            pe.wait_ge(S["span_max"], 1)
            turn_(bank[5][0:1, 128:128 + TJ * 2 * W11], span_t[:, :],
                  ident[0:TJ * 2 * W11, 0:TJ * 2 * W11]).then_inc(S["span_row"], 1)
            pe.wait_ge(S["ld_x"], 32)
            pe.wait_ge(S["pads_set"], 6)
            pe.wait_ge(S["ranges_set"], 1)
            for c in range(3):
                for i in range(4 * c, min(NW, 4 * c + 4)):
                    last = turn_(bank[5 + c][:, (i % 4) * P:(i % 4 + 1) * P], xw[:, i, C3:D], ident[:, :])
                last.then_inc(S["s_turned"], 1)
            pe.wait_ge(S["ld_weights"], 16 * 12)
            for c, (lo, hi) in enumerate(THIRDS):
                pe.wait_ge(S["s_taken"], c + 1)
                mm(bank[5 + c][:, 0:hi - lo], w1[:, :], sT[:, lo:hi], start=True, stop=True).then_inc(S["z_made"], 1)
            pe.wait_ge(S["h_made"], 3)
            turn_(bank[6][:, 0:C], u_sb[:, :], ident[:, :]).then_inc(S["uv_turned"], 1)
            pe.wait_ge(S["uv_taken"], 1)
            mm(bank[7][:, 0:C], uT[:, :], v_sb[:, :], start=True, stop=True).then_inc(S["uv_made"], 1)
            pe.wait_ge(S["edges_taken"], 6)
            pe.wait_ge(S["picks_made"], 2)
            pe.wait_ge(S["uv_set"], 1)

            def spread(i):
                pe.wait_ge(rc_loaded, 32 * (i + 1))
                for k in range(2):
                    if i:
                        pe.wait_ge(S[("turn_made", "wave_scaled")[k]], i)
                    for b in range(PB):
                        last = mm(psum[0:RROWS, k * PB + b, 0:PW], pick[:, k].rearrange("p n c -> p (n c)"),
                                  rc_piece[:, k, b * PW:(b + 1) * PW], start=True, stop=True)
                    last.then_inc(S["rc_spread"], 1)

            def filter_of(w):
                if w >= 2:
                    pe.wait_ge(S["table_rest_made"], w - 1)
                mm(bank[6 + w % 2][:, 0:C3], hT[:, w * P:(w + 1) * P], w3[:, :], start=True, stop=False)
                mm(bank[6 + w % 2][:, 0:C3], ones_row[:, :], b3r[:, :], start=False, stop=True).then_inc(S["filter_made"], 1)

            for i in range(PIECES):
                spread(i)
                for w in (2 * i, 2 * i + 1):
                    if w < NW:
                        filter_of(w)

            def basis(t, q):
                for j in (2 * q, 2 * q + 1):
                    last = mm(bank[j][:, 0:C3], radial[0:RROWS + 3, bass.ds((t + j) * P, P)], w2s[:, :], start=True, stop=True)
                last.then_inc(basis_made[q], 1)

            pe.wait_ge(S["parts_moved"], 16 * PARTS * PIECES)
            pe.wait_ge(S["w2_moved"], 16 * (PARTS + 3))
            pe.wait_ge(S["table_rest_made"], NW)
            pe.wait_ge(S["wave_scaled"], PIECES)
            turns = pe.alloc_register("summed_group_turn")
            over = pe.alloc_register("past_the_window")
            pe.reg_mov(turns, 1)
            t0 = pe.value_load(rng[0:1, 0:1], min_val=0, max_val=NT - 1)
            for q in range(2):
                basis(t0, q)
            with pe.Fori(0, NW) as w:
                first, end = window_range(pe, w)
                first_next = pe.value_load(rng[0:1, bass.ds(w + 1, 1)], min_val=0, max_val=NT - 1)
                pe.wait_ge(S["banks_free"], 2 * w + 1)
                mm(bank[4], zeros_bf[:, 0:P], zeros_bf[:, :], start=True, stop=True, skip_group_check=True)
                pe.wait_ge(S["banks_free"], 2 * w + 2)
                for b in range(3):
                    mm(bank[5 + b][:, 0:CB], zeros_bf[:, 0:P], zeros_bf[:, 0:CB], start=True, stop=True, skip_group_check=True)
                with pe.Fori(first, end, TJ) as t:
                    n1 = pe.snap(turns)
                    pe.reg_alu(over, t + TJ, end, ALU.is_ge)
                    o = pe.snap(over)
                    nxt = pe.snap(t + TJ + o * (first_next - t - TJ), min_val=0, max_val=NT - 1)
                    for q in range(2):
                        for j in (2 * q, 2 * q + 1):
                            pe.wait_ge(hot_made[j], n1)
                            pe.wait_ge(sign_made[j % 2], 2 * n1 - 1 + j // 2)
                            for b in range(3):
                                last = mm(bank[5 + b][:, 0:CB], onehot_bf[:, j, :], sign[:, j % 2, b * CB:(b + 1) * CB],
                                          start=False, stop=True, skip_group_check=True)
                            last.then_inc(sign_used[j % 2], 1)
                            pe.wait_ge(msg_made[j], n1 * 4)
                            mm(bank[4], onehot[:, j, :], msg[:, j, 0:D], start=False, stop=True,
                               skip_group_check=True).then_inc(summed[j], 1)
                        basis(nxt, q)
                    pe.reg_add(turns, turns, 1)
                mm(bank[4], zeros_bf[:, 0:P], zeros_bf[:, :], start=False, stop=True, skip_group_check=True
                   ).then_inc(S["window_summed"], 1)

            for w in range(NW):
                b = w % 2
                pe.wait_ge(S["node_added"], w + 1)
                if w >= 2:
                    pe.wait_ge(S["x1T_taken"], w - 1)
                for i in range(4):
                    last = turn_(bank[b][:, i * P:(i + 1) * P], x1[:, w, i * P:(i + 1) * P], ident[:, :])
                last.then_inc(S["x1T_turned"], 1)
                pe.wait_ge(S["counts_float"], w + 2)
                for c in range(3):
                    m = 3 * w + c
                    if m >= 2:
                        pe.wait_ge(S["counts_taken"], m - 1)
                    for k in range(4 * c, min(NW, 4 * c + 4)):
                        last = turn_(bank[6 + m % 2][:, (k % 4) * P:(k % 4 + 1) * P], counts_f[:, k * P:(k + 1) * P], ident[:, :])
                    last.then_inc(S["counts_turned"], 1)
                pe.wait_ge(S["x1T_taken"], w + 1)
                if w >= 2:
                    pe.wait_ge(S["v_squared"], w - 1)
                for i in range(3):
                    lhs = x1T[:, b, i * C:(i + 1) * C]
                    mm(bank[2 + b][:, i * C:(i + 1) * C], lhs, u_sb[:, :], start=True, stop=True)
                    last = mm(bank[4 + b][:, i * C:(i + 1) * C], lhs, uv_sb[:, :], start=True, stop=True)
                last.then_inc(S["v_made"], 1)
            pe.wait_ge(S["v_squared"], NW)
            pe.wait_ge(S["counts_taken"], 3 * NW)
            for w in range(NW):
                pe.wait_ge(S["norm_made"], w + 1)
                turn_(bank[5 + w // 4][:, (w % 4) * P:(w % 4 + 1) * P], nrm[:, w, :], ident[:, :]).then_inc(S["norm_turned"], 1)
            pe.wait_ge(S["s1_taken"], NW)
            for c, (lo, hi) in enumerate(THIRDS):
                pe.wait_ge(S["norm_taken"], c + 1)
                mm(bank[c][:, 0:hi - lo], wu1[:, 0, :], nT[:, lo:hi], start=True, stop=False)
                mm(bank[c][:, 0:hi - lo], wu1[:, 1, :], sT1[:, lo:hi], start=False, stop=True).then_inc(S["z1_made"], 1)

            def second_messages(d, s):
                n = P if s < NFULL else NTAIL
                return mm(bank[out_bank(d)], countsT[0:n, s, d * P:(d + 1) * P], x1[0:n, s, :],
                          start=(s == 0), stop=(s == NW - 1))

            pe.wait_ge(S["norm_taken"], 3)
            for w in range(NW + 1):
                if w < NW:
                    pe.wait_ge(S["h1_made"], w // 4 + 1)
                    if w >= 2:
                        pe.wait_ge(S["gate_taken"], w - 1)
                    mm(bank[3 + w % 2][:, 0:C3], h1T[:, w * P:(w + 1) * P], wu2[:, :], start=True, stop=False)
                    mm(bank[3 + w % 2][:, 0:C3], ones_row[:, :], bu2r[:, :], start=False, stop=True).then_inc(S["gate_made"], 1)
                if w:
                    pe.wait_ge(S["update_made"], 2 * w)
                    for d in range(EARLY):
                        last = second_messages(d, w - 1)
                        if w == NW:
                            last.then_inc(S["window_done"], 1)
            pe.wait_ge(S["gate_taken"], NW)
            for d in range(EARLY, NW):
                if d >= EARLY + 4:
                    pe.wait_ge(S["res_made"], d - 3)
                for s in range(NW):
                    last = second_messages(d, s)
                last.then_inc(S["window_done"], 1)


_INS = ['x', 'src', 'dst', 'edge_attr_3', 'edge_weight', 'L0_gnn_W1', 'L0_gnn_b1', 'L0_gnn_W2', 'L0_gnn_b2',
        'L0_gnn_W3', 'L0_gnn_b3', 'L0_gnn_U', 'L0_gnn_V', 'L0_gnn_Wu1', 'L0_gnn_bu1', 'L0_gnn_Wu2', 'L0_gnn_bu2']


def kernel(**inputs):
    import concourse.bacc as bacc
    from concourse.bass_utils import run_bass_kernel_spmd

    nc = bacc.Bacc("TRN2", target_bir_lowering=False, num_devices=1)
    arrays, args = {}, []
    for name in _INS:
        a = np.ascontiguousarray(inputs[name])
        arrays[f"in_{name}"] = a
        args.append(nc.dram_tensor(f"in_{name}", a.shape, mybir.dt.from_np(a.dtype), kind="ExternalInput").ap())
    out = nc.dram_tensor("out", inputs["x"].shape, F32, kind="ExternalOutput").ap()
    build(nc, *args, out)
    r = run_bass_kernel_spmd(nc, [arrays], core_ids=[0])
    return r.results[0]["out"]
```

```python
from contextlib import ExitStack

import concourse.bass as bass
from concourse import mybir
import numpy as np

F32 = mybir.dt.float32
BF16 = mybir.dt.bfloat16
I32 = mybir.dt.int32
U16 = mybir.dt.uint16
F16 = mybir.dt.float16
ALU = mybir.AluOpType
ACT = mybir.ActivationFunctionType
AX = mybir.AxisListType

P = 128
R_CUT = 1.4415
N_RBF = 20
EPS = 1e-5
MAGIC = 1.5 * 2.0 ** 23
TWO_ONES = float(np.array([0x3F803F80], np.uint32).view(np.float32)[0])
TWO_PI = float(np.nextafter(np.float32(2 * np.pi), np.float32(0)))
TJ = 4
GE = TJ * P
PARTS = 6
STACK = (0, 0, 0, 1, 1, 2)
STACK_W = (0, 1, 2, 0, 1, 0)
CHUNKS = 6
PIECES = 6
PB = 3


def build(nc, x, src, dst, ea, ew, W1, b1, W2, b2, W3, b3, U, V, Wu1, bu1, Wu2, bu2, out):
    N, D = x.shape
    E = src.shape[0]
    C = W1.shape[0]
    C3 = 3 * C
    TW = C3 + 2 * C
    NW = -(-N // P)
    NFULL = N // P
    NTAIL = N - NFULL * P
    NT = -(-E // P)
    NGF = E // GE
    ETAIL = E - NGF * GE
    GR = 81
    NPAD = NW * P
    RROWS = CHUNKS * N_RBF
    CH = GR * GE // CHUNKS
    PC = CH // PIECES
    PW = PC // PB
    GW = CHUNKS * CH
    NC1 = N + 1
    CB = NC1 // 3
    W11 = NW + 1
    assert CHUNKS * PIECES * PB * PW == GR * GE and (NT + TJ - 1) * P <= GW and C == P and 3 * CB == NC1
    assert PARTS * N_RBF == RROWS

    node_table = nc.dram_tensor("node_table", (NPAD, TW), F32, kind="Internal").ap()
    rc_rows = nc.dram_tensor("rc_rows", (2, GR * GE), F32, kind="Internal").ap()
    part_rows = nc.dram_tensor("part_rows", (3, RROWS, CH), BF16, kind="Internal").ap()

    with ExitStack() as ctx:
        def sb(name, shape, dt=F32):
            return ctx.enter_context(nc.sbuf_tensor(name, shape, dt))

        def sem(name):
            return ctx.enter_context(nc.semaphore(name))

        psum = ctx.enter_context(nc.psum_tensor("psum", [P, 8, 512], F32))
        bank = [psum[:, i, :] for i in range(8)]

        class Region:

            def __init__(self, ap, width):
                self.ap, self.width, self.at = ap, width, 0

            def cut(self, width, dt=F32, rows=P):
                words = width if dt in (F32, I32) else -(-width // 2)
                a = self.ap[0:rows, self.at:self.at + words]
                self.at += words
                assert self.at <= self.width
                if dt in (BF16, F16, U16):
                    return a.bitcast(dt)[:, 0:width]
                return a if dt == F32 else a.bitcast(dt)

        radial = sb("radial", [P, GW], BF16)
        work = sb("work", [P, NW * D + 2 * TJ * TW])
        side = sb("side", [P, 9328])

        def regions():
            return (Region(radial[:, :].bitcast(F32), GW // 2), Region(work, NW * D + 2 * TJ * TW), Region(side, 9328))

        ident = sb("ident", [P, P])
        node_no = sb("node_no", [P, NPAD + 2], F16)
        ones_row = sb("ones_row", [1, P])
        zeros_bf = sb("zeros_bf", [P, 512], BF16)
        w1 = sb("w1", [P, C])
        w3 = sb("w3", [P, C3])
        u_sb = sb("u_sb", [P, C])
        v_sb = sb("v_sb", [P, C])
        uv_sb = sb("uv_sb", [P, C])
        wu1 = sb("wu1", [P, 2, C])
        wu2 = sb("wu2", [P, C3])
        b1c = sb("b1c", [P, 1])
        bu1c = sb("bu1c", [P, 1])
        b3r = sb("b3r", [1, C3])
        bu2r = sb("bu2r", [1, C3])
        w2s = sb("w2s", [RROWS + 3, C3], BF16)
        pick = sb("pick", [CHUNKS, 2, N_RBF, CHUNKS])
        half_pi = sb("half_pi", [GR, 1])
        count_bias = sb("count_bias", [P, 1])

        xw = sb("xw", [P, NW, D])
        dst_c = sb("dst_c", [P, GR * TJ], F16)
        src_c = sb("src_c", [P, GR * TJ], I32)
        src_b = sb("src_b", [P, GR * TJ])
        ea_c = sb("ea_c", [P, 3, GR * TJ])
        idx = sb("idx", [P, 2, TJ], I32)
        onehot = sb("onehot", [P, TJ, P])
        sign = sb("sign", [P, 2, NC1 + 1], BF16)
        onehot_bf = sb("onehot_bf", [P, TJ, P], BF16)
        rng = sb("rng", [1, 2 * W11], I32)

        r_rad, r_work, r_side = regions()
        w2f = r_rad.cut(C3, rows=N_RBF)
        b2f = r_rad.cut(C3, rows=1)
        w2p = r_rad.cut(3 * C3, BF16, rows=N_RBF).rearrange("p (k f) -> p k f", k=3)
        b2p = r_rad.cut(3 * C3, BF16, rows=1).rearrange("p (k f) -> p k f", k=3)
        node_no_i = r_rad.cut(NPAD + 2, I32)
        pick_i = r_rad.cut(2 * RROWS, I32, rows=CHUNKS).rearrange("p (k n c) -> p k n c", k=2, n=N_RBF)
        src_i = r_work.cut(GE, I32, rows=GR)
        dst_i = r_work.cut(GE, I32, rows=GR)
        dst_hi_i = r_work.cut(GE, I32, rows=GR)
        ea_r = r_work.cut(3 * GE, rows=GR)
        r_r = r_work.cut(GE, rows=GR)
        src_f = r_work.cut(GE, rows=GR)
        dst_f = r_work.cut(GE, rows=GR)
        coef = r_work.cut(GE, rows=GR)
        tmp_a = r_work.cut(GE, rows=GR)
        tmp_b = r_work.cut(GE, rows=GR)
        sT = r_work.cut(NPAD)
        hT = r_work.cut(NPAD)
        table_out = r_work.cut(2 * TW).rearrange("p (b f) -> p b f", b=2)
        turn = r_side.cut(PC, rows=RROWS).rearrange("p (b f) -> p b f", b=PB)
        wave = r_side.cut(2 * PC, rows=RROWS).rearrange("p (d f) -> p d f", d=2)
        part = r_side.cut(6 * PC, BF16, rows=RROWS).rearrange("p (d k f) -> p d k f", d=2, k=3)
        rc_piece = r_side.cut(2 * PC, rows=CHUNKS).rearrange("p (k f) -> p k f", k=2)
        first_filter = onehot[:, 0:2, :]
        uT = sT[:, 0:C]
        tile_no_i = r_work.cut(TJ, I32, rows=GR)
        tile_no = r_work.cut(TJ, rows=GR)
        win_lo_i = r_work.cut(W11, I32, rows=GR)
        win_lo = r_work.cut(W11, rows=GR)
        least = r_work.cut(TJ, rows=GR)
        most = r_work.cut(TJ, rows=GR)
        to_last = r_work.cut(TJ, rows=GR)
        past = r_work.cut(TJ, rows=GR)
        in_span = r_work.cut(W11, rows=GR)
        span = r_work.cut(TJ * 2 * W11, rows=GR).rearrange("p (j k w) -> p j k w", j=TJ, k=2)
        rng_f = r_work.cut(2 * W11, rows=1).rearrange("p (k w) -> p k w", k=2)
        span_t = r_work.cut(1, rows=TJ * 2 * W11)

        r_rad, r_work, r_side = regions()
        x1 = r_work.cut(NW * D).rearrange("p (w f) -> p w f", w=NW)
        rows = r_work.cut(2 * TJ * TW).rearrange("p (h j f) -> p h j f", h=2, j=TJ)
        cumul = r_side.cut(NW * (NC1 + 1), U16).rearrange("p (w f) -> p w f", w=NW)

        r_rad, r_work, r_side = regions()
        countsT = r_rad.cut(NW * NPAD).rearrange("p (s d) -> p s d", s=NW)
        vu = r_rad.cut(NW * C3).rearrange("p (w f) -> p w f", w=NW)
        vv = r_rad.cut(NW * C3).rearrange("p (w f) -> p w f", w=NW)
        r_work.cut(NW * D)
        x1T = r_work.cut(2 * D).rearrange("p (b f) -> p b f", b=2)
        sT1 = r_work.cut(NPAD)
        nrm = r_work.cut(NPAD).rearrange("p (w f) -> p w f", w=NW)
        nT = r_work.cut(NPAD)
        r_side.cut(NW * (NC1 + 1), U16)
        h1T = r_side.cut(NPAD)
        counts_f = r_side.cut(NPAD)
        sq = r_side.cut(C3)
        stat = r_side.cut(NW * 12).rearrange("p (w f) -> p w f", w=NW)
        ssq = r_work.cut(2 * C).rearrange("p (b f) -> p b f", b=2)
        prod, dot = sq, ssq[:, 0, :]
        y = x1T
        hh = x1T[:, :, 0:C3]

        names = """ld_x ld_r ld_edges ld_w2 ld_weights pads_set pool_const picks_made dve_const half_pi_set dve_step cos_in
        cos_done rc_made rc_stored rc_spread turn_made sin_done wave_scaled hi_made wave_less_hi mid_made lo_made
        parts_moved w2_split w2_moved edges_float edges_turned edges_taken span_made span_turned span_max span_row
        ranges_set s_turned s_taken z_made sig_made h_made filter_made filter_taken table_vec_made table_rest_made
        uv_turned uv_taken uv_made uv_set window_summed sums_flushed counts_flushed
        node_added x1T_turned x1T_taken v_made v_taken v_squared norm_sq norm_made norm_turned norm_taken s1_taken
        z1_made sig1_made h1_made gate_made gate_taken update_made counts_float counts_turned counts_taken
        window_done res_made ln_stats ln_mean var_made std_made ln_scale y_made y_stored turn_read x_residual""".split()
        S = {n: sem(n) for n in names}
        rc_loaded = sem("rc_loaded")
        parts_stored = [sem(f"parts_stored{b}") for b in range(2)]
        table_stored = [sem(f"table_stored{b}") for b in range(2)]
        gathered = [[sem(f"gathered{h}_{j}") for j in range(TJ)] for h in range(2)]
        indices_set = [[sem(f"indices_set{h}_{q}") for q in range(2)] for h in range(2)]
        products_made = [sem(f"products_made{q}") for q in range(2)]
        basis_made = [sem(f"basis_made{q}") for q in range(2)]
        hot_made = [sem(f"hot_made{q}") for q in range(2)]
        hot_widened = [sem(f"hot_widened{q}") for q in range(2)]
        msg_made = [sem(f"msg_made{j}") for j in range(TJ)]
        summed = [sem(f"summed{j}") for j in range(TJ)]
        sign_made = [sem(f"sign_made{b}") for b in range(2)]
        sign_used = [sem(f"sign_used{b}") for b in range(2)]
        THIRDS = ((0, 512), (512, 1024), (1024, NPAD))

        EARLY = 3

        def out_bank(w):
            return 5 + w if w < EARLY else (w - EARLY) % 4

        def through(n, b):
            return (n + 1 - b) // 2

        def window_range(eng, w):
            first = eng.value_load(rng[0:1, bass.ds(w, 1)], min_val=0, max_val=NT - 1)
            end = eng.value_load(rng[0:1, bass.ds(w + W11, 1)], min_val=1, max_val=NT)
            return first, end

        block = ctx.enter_context(nc.Block())

        @block.sync
        def _(sp):
            def load_rows(a, b_, width, done):
                sp.dma_start(a[0:NGF, :], b_[0:NGF * GE * width].rearrange("(g f) -> g f", f=GE * width)).then_inc(done, 16)
                sp.dma_start(a[NGF:NGF + 1, 0:ETAIL * width],
                             b_[NGF * GE * width:E * width].rearrange("(g f) -> g f", g=1)).then_inc(done, 16)

            sp.dma_start(w2f, W2).then_inc(S["ld_w2"], 16)
            sp.dma_start(b2f, b2.rearrange("(a f) -> a f", a=1)).then_inc(S["ld_w2"], 16)
            sp.wait_ge(S["pads_set"], 1)
            load_rows(r_r, ew, 1, S["ld_r"])
            sp.wait_ge(S["pads_set"], 6)
            for a, b_, width in ((dst_i, dst, 1), (dst_hi_i, dst, 1), (src_i, src, 1), (ea_r, ea.rearrange("e k -> (e k)"), 3)):
                load_rows(a, b_, width, S["ld_edges"])
            sp.dma_start(xw[:, 0:NFULL, :], x[0:NFULL * P, :].rearrange("(w p) f -> p w f", p=P)).then_inc(S["ld_x"], 16)
            sp.dma_start(xw[0:NTAIL, NFULL, :], x[NFULL * P:N, :]).then_inc(S["ld_x"], 16)
            for a, b_ in ((w1[:, :], W1), (w3[:, :], W3), (b1c[:, :], b1.rearrange("(p a) -> p a", a=1)),
                          (b3r[:, :], b3.rearrange("(a f) -> a f", a=1)), (u_sb[:, :], U), (v_sb[:, :], V),
                          (wu1[:, :, :], Wu1.rearrange("(k p) f -> p k f", p=P)),
                          (bu1c[:, :], bu1.rearrange("(p a) -> p a", a=1)), (wu2[:, :], Wu2),
                          (bu2r[:, :], bu2.rearrange("(a f) -> a f", a=1))):
                sp.dma_start(a, b_).then_inc(S["ld_weights"], 16)
            sp.wait_ge(S["w2_split"], 2)
            for q, k in enumerate(STACK_W):
                sp.dma_start(w2s[q * N_RBF:(q + 1) * N_RBF, :], w2p[:, k, :]).then_inc(S["w2_moved"], 16)
            for k in range(3):
                sp.dma_start(w2s[RROWS + k:RROWS + k + 1, :], b2p[:, k, :]).then_inc(S["w2_moved"], 16)
            sp.wait_ge(S["rc_made"], 1)
            sp.dma_start(rc_rows[0].rearrange("(g f) -> g f", f=GE), r_r).then_inc(S["rc_stored"], 16)
            sp.dma_start(rc_rows[1].rearrange("(g f) -> g f", f=GE), coef).then_inc(S["rc_stored"], 16)
            sp.wait_ge(S["rc_stored"], 32)

            def load_piece(i):
                if i:
                    sp.wait_ge(S["rc_spread"], 2 * i)
                for k in range(2):
                    sp.dma_start(rc_piece[:, k, :], rc_rows[k, 0:GW].rearrange("(c f) -> c f", c=CHUNKS)[:, i * PC:(i + 1) * PC]
                                 ).then_inc(rc_loaded, 16)

            def store_table(w):
                sp.wait_ge(S["table_vec_made"], w + 1)
                sp.wait_ge(S["table_rest_made"], w + 1)
                sp.dma_start(node_table[w * P:(w + 1) * P, :], table_out[:, w % 2, :]).then_inc(table_stored[w % 2], 16)

            def load_stack(i):
                sp.wait_ge(parts_stored[i % 2], 16 * (i // 2 + 1))
                if i:
                    sp.wait_ge(S["parts_moved"], 16 * PARTS * i)
                else:
                    sp.wait_ge(S["pads_set"], 7)
                for q, k in enumerate(STACK):
                    sp.dma_start(radial[q * N_RBF:(q + 1) * N_RBF, :].rearrange("p (c f) -> p c f", c=CHUNKS)[:, :, i * PC:(i + 1) * PC],
                                 part_rows[k].rearrange("(n c) f -> n c f", c=CHUNKS)[:, :, i * PC:(i + 1) * PC]
                                 ).then_inc(S["parts_moved"], 16)

            load_piece(0)
            load_piece(1)
            for i in range(PIECES):
                if i + 2 < PIECES:
                    load_piece(i + 2)
                for w in (2 * i, 2 * i + 1):
                    if w < NW:
                        store_table(w)
                sp.wait_ge(S["lo_made"], i + 1)
                sp.dma_start(part_rows[:, :, i * PC:(i + 1) * PC].rearrange("k p f -> p k f"), part[:, i % 2, :, :]
                             ).then_inc(parts_stored[i % 2], 16)
                if i:
                    load_stack(i - 1)
            load_stack(PIECES - 1)
            for w in range(NW):
                n = P if w < NFULL else NTAIL
                sp.wait_ge(S["y_made"], w + 1)
                sp.dma_start(out[w * P:w * P + n, :], xw[0:n, w, :]).then_inc(S["y_stored"], 16)
            sp.wait_ge(S["y_stored"], 16 * NW)

        @block.gpsimd
        def _(pool):
            g = nc.gpsimd
            g.memset(r_r, 1.0).then_inc(S["pads_set"], 1)
            g.memset(dst_i, -1).then_inc(S["pads_set"], 1)
            g.memset(dst_hi_i, 2 * NPAD).then_inc(S["pads_set"], 1)
            g.memset(src_i, 0).then_inc(S["pads_set"], 1)
            g.memset(ea_r, 0.0).then_inc(S["pads_set"], 1)
            g.memset(xw[:, NFULL, :], 0.0).then_inc(S["pads_set"], 1)
            g.iota(pick_i[:, 0], pattern=[[1, N_RBF], [0, CHUNKS]], base=1, channel_multiplier=0).then_inc(S["pool_const"], 1)
            g.iota(pick_i[:, 1], pattern=[[0, N_RBF], [1, CHUNKS]], base=0, channel_multiplier=-1).then_inc(S["pool_const"], 1)
            g.memset(ident[:, :], 0.0).then_inc(S["pool_const"], 1)
            pool.wait_ge(S["pool_const"], 3)
            g.affine_select(out=ident[:, :], in_=ident[:, :], compare_op=ALU.not_equal, fill=1.0, base=0,
                            pattern=[[-1, P]], channel_multiplier=1).then_inc(S["pool_const"], 1)
            g.iota(tile_no_i[:, :], pattern=[[1, TJ]], base=0, channel_multiplier=TJ).then_inc(S["pool_const"], 1)
            g.iota(win_lo_i[:, :], pattern=[[P, W11]], base=0, channel_multiplier=0).then_inc(S["pool_const"], 1)
            g.iota(node_no_i, pattern=[[1, NPAD + 2]], base=-2, channel_multiplier=0).then_inc(S["pool_const"], 1)
            pool.wait_ge(S["dve_const"], 3)
            pool.wait_ge(S["picks_made"], 2)
            pool.wait_ge(S["w2_moved"], 16 * (PARTS + 3))
            g.memset(radial[96:P, :].bitcast(F32), TWO_ONES).then_inc(S["pads_set"], 1)
            pool.wait_ge(S["pads_set"], 7)
            for i in range(PIECES):
                b = i % 2
                pool.wait_ge(S["hi_made"], i + 1)
                g.tensor_tensor(wave[:, b, :], wave[:, b, :], part[:, b, 0, :], ALU.subtract).then_inc(S["wave_less_hi"], 1)
                pool.wait_ge(S["mid_made"], i + 1)
                g.tensor_tensor(part[:, b, 2, :], wave[:, b, :], part[:, b, 1, :], ALU.subtract).then_inc(S["lo_made"], 1)

            turns = pool.alloc_register("group_after")
            half_turns = [pool.alloc_register(f"turns_of_half{h}") for h in range(2)]
            half_free = [pool.alloc_register(f"half{h}_is_free") for h in range(2)]
            pool.reg_mov(turns, 2)
            half = pool.alloc_register("half_to_gather_to")
            pool.reg_mov(half, 0)
            for h in range(2):
                pool.reg_mov(half_turns[h], 1)
                pool.reg_mov(half_free[h], 1)
            pool.wait_ge(S["ranges_set"], 1)
            pool.wait_ge(S["edges_taken"], 6)
            pool.wait_ge(S["lo_made"], PIECES)
            for b in range(2):
                pool.wait_ge(table_stored[b], 16 * through(NW, b))

            def gathers(t, h):
                turn_h = pool.snap(half_turns[h])
                free_h = pool.snap(half_free[h])
                at = pool.snap(t, min_val=0, max_val=NT + TJ - 1)
                for q in range(2):
                    pool.wait_ge(S["ranges_set"], 1)
                    pool.wait_ge(summed[2 * q], free_h)
                    pool.wait_ge(summed[2 * q + 1], free_h)
                    g.tensor_copy(idx[:, h, 2 * q:2 * q + 2], src_c[:, bass.ds(at + 2 * q, 2)]).then_inc(indices_set[h][q], 1)
                    for j in (2 * q, 2 * q + 1):
                        pool.wait_ge(S["ranges_set"], 1)
                        if j == 2 * q:
                            pool.wait_ge(indices_set[h][q], turn_h)
                        g.indirect_dma_start(
                            out=rows[:, h, j, :], out_offset=None, in_=node_table,
                            in_offset=bass.IndirectOffsetOnAxis(ap=idx[:, h, j:j + 1], axis=0)).then_inc(gathered[h][j], 16)
                pool.reg_add(half_turns[h], half_turns[h], 1)
                pool.reg_mov(half_free[h], turns)
                pool.reg_add(turns, turns, 1)
                pool.reg_mov(half, 1 - h)

            with pool.Fori(0, NW) as w:
                first, end = window_range(pool, w)
                in_half = pool.snap(half)
                for h in range(2):
                    with pool.If(in_half == h):
                        with pool.Fori(first, end, 2 * TJ) as t:
                            gathers(t, h)
                            with pool.If(t + TJ < end):
                                gathers(t + TJ, 1 - h)
            pool.wait_ge(S["counts_flushed"], NW + 1)
            pool.wait_ge(S["sums_flushed"], NW + 1)
            g.memset(counts_f[:, N:NPAD], 0.0).then_inc(S["counts_float"], 1)
            for w in range(NW):
                g.tensor_tensor(x1[:, w, :], x1[:, w, :], xw[:, w, :], ALU.add).then_inc(S["node_added"], 1)
                pool.wait_ge(S["node_added"], w + 1)
                g.tensor_tensor(xw[:, w, :], xw[:, w, :], x1[:, w, :], ALU.add).then_inc(S["x_residual"], 1)

        @block.scalar
        def _(act):
            a = nc.scalar
            act.sem_inc(S["sums_flushed"], 1)
            act.sem_inc(S["counts_flushed"], 1)
            act.wait_ge(S["cos_in"], 1)
            act.wait_ge(S["half_pi_set"], 1)
            a.activation(tmp_b, tmp_a, ACT.Sin, bias=half_pi[:, :], scale=-float(np.pi / R_CUT)).then_inc(S["cos_done"], 1)
            for c, (lo, hi) in enumerate(THIRDS):
                act.wait_ge(S["z_made"], c + 1)
                a.activation(hT[:, lo:hi], bank[5 + c][:, 0:hi - lo], ACT.Sigmoid, bias=b1c[:, :]).then_inc(S["sig_made"], 1)

            def take_filter(w):
                b = w % 2
                act.wait_ge(S["filter_made"], w + 1)
                if w >= 2:
                    act.wait_ge(table_stored[b], 16 * (w // 2))
                    act.wait_ge(S["table_vec_made"], w - 1)
                a.copy(first_filter[:, b, :], bank[6 + b][:, 0:C]).then_inc(S["filter_taken"], 1)
                a.copy(table_out[:, b, C3:TW], bank[6 + b][:, C:C3]).then_inc(S["table_rest_made"], 1)

            def middle(i):
                act.wait_ge(S["wave_less_hi"], i + 1)
                a.copy(part[:, i % 2, 1, :], wave[:, i % 2, :]).then_inc(S["mid_made"], 1)

            for i in range(PIECES):
                b = i % 2
                act.wait_ge(S["turn_made"], i + 1)
                if i >= 2:
                    act.wait_ge(S["lo_made"], i - 1)
                a.activation(wave[:, b, :], turn[:, :, :].rearrange("p b f -> p (b f)"), ACT.Sin, scale=TWO_PI
                             ).then_inc(S["sin_done"], 1)
                if i:
                    middle(i - 1)
                act.wait_ge(S["wave_scaled"], i + 1)
                if i >= 2:
                    act.wait_ge(parts_stored[b], 16 * (i // 2))
                a.copy(part[:, b, 0, :], wave[:, b, :]).then_inc(S["hi_made"], 1)
                for w in (2 * i, 2 * i + 1):
                    if w < NW:
                        take_filter(w)
            middle(PIECES - 1)

            turns = act.alloc_register("signed_group_turn")
            act.reg_mov(turns, 1)
            signs_counted = act.alloc_register("signs_counted")
            act.reg_mov(signs_counted, 1)
            act.wait_ge(S["ranges_set"], 1)
            act.wait_ge(S["half_pi_set"], 2)
            act.wait_ge(S["edges_taken"], 6)
            with act.Fori(0, NW) as w:
                first, end = window_range(act, w)
                with act.Fori(first, end, TJ) as t:
                    n1 = act.snap(turns)
                    for j in range(TJ):
                        b = j % 2
                        act.wait_ge(sign_used[b], 2 * n1 - 1 + j // 2)
                        a.activation(sign[:, b, 0:NC1], node_no[:, 1:1 + NC1], ACT.Sign,
                                     bias=src_b[:, bass.ds(t + j, 1)]).then_inc(sign_made[b], 1)
                        if j % 2:
                            act.wait_ge(hot_made[j // 2], n1)
                            a.copy(onehot[:, j - 1:j + 1, :], onehot_bf[:, j - 1:j + 1, :]).then_inc(hot_widened[j // 2], 1)
                    act.reg_add(turns, turns, 1)
                    act.reg_add(signs_counted, signs_counted, TJ // 2)
                act.wait_ge(S["lo_made"], PIECES)
                for b in range(2):
                    act.wait_ge(parts_stored[b], 16 * through(PIECES, b))
                counted = act.snap(signs_counted)
                for b in range(2):
                    act.wait_ge(sign_used[b], counted)
                a.activation(cumul[:, bass.ds(w, 1), 0:NC1].rearrange("p a (b f) -> p (a b) f", b=3), psum[:, 5:8, 0:CB],
                             ACT.Identity, bias=count_bias[:, :], scale=0.5).then_inc(S["counts_flushed"], 1)
                act.wait_ge(S["window_summed"], w + 1)
                a.copy(x1[:, bass.ds(w, 1), :], bank[4].unsqueeze(1)).then_inc(S["sums_flushed"], 1)

            for w in range(NW):
                b = w % 2
                act.wait_ge(S["x1T_turned"], w + 1)
                if w >= 2:
                    act.wait_ge(S["v_made"], w - 1)
                    act.wait_ge(S["s1_taken"], w - 1)
                a.copy(x1T[:, b, :], bank[b]).then_inc(S["x1T_taken"], 1)
                act.wait_ge(S["v_made"], w + 1)
                a.copy(vu[:, w, :], bank[2 + b][:, 0:C3]).then_inc(S["v_taken"], 1)
                a.copy(vv[:, w, :], bank[4 + b][:, 0:C3]).then_inc(S["v_taken"], 1)
                if w:
                    act.wait_ge(S["norm_sq"], w)
                a.activation(sq[:, :], bank[4 + b][:, 0:C3], ACT.Square).then_inc(S["v_squared"], 1)
                if w:
                    act.wait_ge(S["norm_sq"], w)
                    a.activation(nrm[:, w - 1, :], ssq[:, (w - 1) % 2, :], ACT.Sqrt).then_inc(S["norm_made"], 1)
            act.wait_ge(S["norm_sq"], NW)
            a.activation(nrm[:, NW - 1, :], ssq[:, (NW - 1) % 2, :], ACT.Sqrt).then_inc(S["norm_made"], 1)
            for c, (lo, hi) in enumerate(THIRDS):
                act.wait_ge(S["z1_made"], c + 1)
                a.activation(h1T[:, lo:hi], bank[c][:, 0:hi - lo], ACT.Sigmoid, bias=bu1c[:, :]).then_inc(S["sig1_made"], 1)
            for w in range(NW):
                act.wait_ge(S["gate_made"], w + 1)
                if w >= 2:
                    act.wait_ge(S["update_made"], 2 * (w - 1))
                a.copy(hh[:, w % 2, :], bank[3 + w % 2][:, 0:C3]).then_inc(S["gate_taken"], 1)
            for w in range(NW):
                act.wait_ge(S["var_made"], w + 1)
                a.activation(stat[:, w, 9:10], stat[:, w, 8:9], ACT.Sqrt).then_inc(S["std_made"], 1)

        @block.vector
        def _(dve):
            v = nc.vector
            steps = [0]

            def then(ins):
                steps[0] += 1
                ins.then_inc(S["dve_step"], 1)
                dve.wait_ge(S["dve_step"], steps[0])

            v.memset(half_pi[:, :], float(np.pi / 2)).then_inc(S["half_pi_set"], 1)
            v.memset(count_bias[:, :], E / 2 + 0.25).then_inc(S["half_pi_set"], 1)
            v.memset(ones_row[:, :], 1.0).then_inc(S["dve_const"], 1)
            v.memset(zeros_bf[:, :], 0.0).then_inc(S["dve_const"], 1)
            dve.wait_ge(S["ld_r"], 32)
            v.tensor_scalar(tmp_a, r_r, R_CUT, None, ALU.min).then_inc(S["cos_in"], 1)
            then(v.reciprocal(coef, r_r))
            dve.wait_ge(S["cos_done"], 1)
            k = 0.5 * float(np.sqrt(np.float32(2.0 / R_CUT)))
            then(v.tensor_scalar(tmp_b, tmp_b, 1.0, k, ALU.add, ALU.mult))
            then(v.scalar_tensor_tensor(out=tmp_b, in0=r_r, scalar=R_CUT, in1=tmp_b, op0=ALU.is_lt, op1=ALU.mult))
            v.tensor_tensor(coef, tmp_b, coef, ALU.mult).then_inc(S["rc_made"], 1)
            dve.wait_ge(S["ld_w2"], 32)
            for full, parts in ((w2f, w2p), (b2f, b2p)):
                then(v.tensor_copy(parts[:, 0, :], full))
                then(v.tensor_tensor(full, full, parts[:, 0, :], ALU.subtract))
                then(v.tensor_copy(parts[:, 1, :], full))
                v.tensor_tensor(parts[:, 2, :], full, parts[:, 1, :], ALU.subtract).then_inc(S["w2_split"], 1)
            dve.wait_ge(S["pool_const"], 7)
            v.tensor_scalar(pick[:, 1], pick_i[:, 1], 0.0, None, ALU.is_equal).then_inc(S["picks_made"], 1)
            dve.wait_ge(S["picks_made"], 1)
            v.scalar_tensor_tensor(out=pick[:, 0], in0=pick_i[:, 0], scalar=1.0 / (2 * R_CUT), in1=pick[:, 1],
                                   op0=ALU.mult, op1=ALU.mult).then_inc(S["picks_made"], 1)
            v.tensor_copy(node_no[:, :], node_no_i).then_inc(S["dve_const"], 1)
            dve.wait_ge(S["ld_edges"], 16 * 8)
            v.tensor_copy(src_f, src_i).then_inc(S["edges_float"], 1)
            dve.wait_ge(S["rc_made"], 1)
            v.tensor_copy(dst_f, dst_i).then_inc(S["edges_float"], 1)
            dve.wait_ge(S["edges_float"], 2)
            then(v.tensor_copy(tmp_a, dst_hi_i))
            then(v.tensor_copy(tile_no[:, :], tile_no_i[:, :]))
            then(v.tensor_copy(win_lo[:, :], win_lo_i[:, :]))
            then(v.tensor_reduce(most[:, :], dst_f.rearrange("g (j f) -> g j f", j=TJ), AX.X, ALU.max))
            then(v.tensor_reduce(least[:, :], tmp_a.rearrange("g (j f) -> g j f", j=TJ), AX.X, ALU.min))
            then(v.tensor_scalar(to_last[:, :], tile_no[:, :], -1.0, float(NT), ALU.mult, ALU.add))
            then(v.tensor_scalar(past[:, :], tile_no[:, :], 1.0, None, ALU.add))
            for j in range(TJ):
                then(v.tensor_scalar(in_span[:, :], win_lo[:, :], float(P - 1), least[:, j:j + 1], ALU.add, ALU.is_ge))
                then(v.scalar_tensor_tensor(out=in_span[:, :], in0=win_lo[:, :], scalar=most[:, j:j + 1], in1=in_span[:, :],
                                            op0=ALU.is_le, op1=ALU.mult))
                v.tensor_scalar(span[:, j, 0, :], in_span[:, :], to_last[:, j:j + 1], -float(NT), ALU.mult,
                                ALU.add).then_inc(S["span_made"], 1)
                v.tensor_scalar(span[:, j, 1, :], in_span[:, :], past[:, j:j + 1], None, ALU.mult).then_inc(S["span_made"], 1)
                dve.wait_ge(S["span_made"], 2 * j + 2)
            dve.wait_ge(S["span_turned"], 1)
            v.tensor_reduce(span_t[:, :], bank[5][0:TJ * 2 * W11, 0:GR], AX.X, ALU.max).then_inc(S["span_max"], 1)
            dve.wait_ge(S["span_row"], 1)
            then(v.tensor_reduce(rng_f[:, :, :].rearrange("p a b -> p (a b)"),
                                 bank[5][0:1, 128:128 + TJ * 2 * W11].rearrange("p (j c) -> p c j", j=TJ), AX.X, ALU.max))
            lo_f, end_f = rng_f[0:1, 0, :], rng_f[0:1, 1, :]
            then(v.tensor_scalar(lo_f, lo_f, -1.0, float(NT - 1), ALU.mult, ALU.min))
            then(v.scalar_tensor_tensor(out=end_f, in0=lo_f, scalar=1.0, in1=end_f, op0=ALU.add, op1=ALU.max))
            v.tensor_copy(rng[:, :], rng_f[:, :, :].rearrange("p a b -> p (a b)")).then_inc(S["ranges_set"], 1)
            dve.wait_ge(S["edges_turned"], 5)

            def columns(ap):
                return ap.rearrange("p (g j) -> p j g", j=TJ)

            def turned(i):
                return bank[i][:, 0:TJ * GR].rearrange("p (j g) -> p j g", j=TJ)

            v.tensor_copy(columns(dst_c[:, :]), turned(0)).then_inc(S["edges_taken"], 1)
            v.tensor_copy(columns(src_c[:, :]), turned(1)).then_inc(S["edges_taken"], 1)
            v.tensor_scalar(columns(src_b[:, :]), turned(1), -1.0, 0.5, ALU.mult, ALU.add).then_inc(S["edges_taken"], 1)
            for c in range(3):
                v.tensor_copy(columns(ea_c[:, c]), turned(2 + c)).then_inc(S["edges_taken"], 1)
            for c, (lo, hi) in enumerate(THIRDS):
                dve.wait_ge(S["s_turned"], c + 1)
                v.tensor_copy(sT[:, lo:hi], bank[5 + c][:, 0:hi - lo]).then_inc(S["s_taken"], 1)
            for c, (lo, hi) in enumerate(THIRDS):
                dve.wait_ge(S["sig_made"], c + 1)
                v.scalar_tensor_tensor(out=hT[:, lo:hi], in0=bank[5 + c][:, 0:hi - lo], scalar=b1c[:, :], in1=hT[:, lo:hi],
                                       op0=ALU.add, op1=ALU.mult).then_inc(S["h_made"], 1)
            dve.wait_ge(S["uv_turned"], 1)
            v.tensor_copy(uT, bank[6][:, 0:C]).then_inc(S["uv_taken"], 1)
            dve.wait_ge(S["uv_made"], 1)
            v.tensor_copy(uv_sb[:, :], bank[7][:, 0:C]).then_inc(S["uv_set"], 1)
            for i in range(PIECES):
                turns_x, coef_x = psum[0:RROWS, 0:PB, 0:PW], psum[0:RROWS, PB:2 * PB, 0:PW]
                dve.wait_ge(S["rc_spread"], 2 * i + 1)
                if i:
                    dve.wait_ge(S["sin_done"], i)
                then(v.tensor_scalar(turn, turns_x, MAGIC, MAGIC, ALU.add, ALU.subtract))
                v.tensor_tensor(turn, turns_x, turn, ALU.subtract).then_inc(S["turn_made"], 1)
                dve.wait_ge(S["sin_done"], i + 1)
                dve.wait_ge(S["rc_spread"], 2 * i + 2)
                wv = wave[:, i % 2, :].rearrange("p (b f) -> p b f", b=PB)
                v.tensor_tensor(wv, wv, coef_x, ALU.mult).then_inc(S["wave_scaled"], 1)
                for w in (2 * i, 2 * i + 1):
                    if w < NW:
                        dve.wait_ge(S["filter_taken"], w + 1)
                        if w >= 2:
                            dve.wait_ge(table_stored[w % 2], 16 * (w // 2))
                        v.tensor_tensor(table_out[:, w % 2, 0:C3].rearrange("p (c k) -> p c k", k=3),
                                        xw[:, w, 0:C3].rearrange("p (c k) -> p c k", k=3),
                                        first_filter[:, w % 2, :].unsqueeze(2).to_broadcast((P, C, 3)),
                                        ALU.mult).then_inc(S["table_vec_made"], 1)

            turns = dve.alloc_register("message_group_turn")
            half_turns = [dve.alloc_register(f"message_turns_of_half{h}") for h in range(2)]
            for reg in [turns] + half_turns:
                dve.reg_mov(reg, 1)
            half = dve.alloc_register("half_of_messages")
            dve.reg_mov(half, 0)

            def messages(w, t, h):
                n1 = dve.snap(turns)
                turn_h = dve.snap(half_turns[h])
                for q in range(2):
                    pair = slice(2 * q, 2 * q + 2)
                    vec = rows[:, h, pair, 0:C3].rearrange("p j (c k) -> p j c k", k=3)
                    dve.wait_ge(gathered[h][2 * q], turn_h * 16)
                    dve.wait_ge(gathered[h][2 * q + 1], turn_h * 16)
                    dve.wait_ge(basis_made[q], n1)
                    v.tensor_tensor(rows[:, h, pair, C3:TW], rows[:, h, pair, C3:TW], psum[:, pair, C:C3],
                                    ALU.mult).then_inc(products_made[q], 1)
                    v.tensor_tensor(vec, vec, psum[:, pair, 0:C].unsqueeze(3).to_broadcast((P, 2, C, 3)),
                                    ALU.mult).then_inc(products_made[q], 1)
                    for j in (2 * q, 2 * q + 1):
                        dve.wait_ge(summed[j], n1)
                    v.tensor_tensor(onehot_bf[:, pair, :], node_no[:, bass.ds(w * P + 2, P)].unsqueeze(1).to_broadcast((P, 2, P)),
                                    dst_c[:, bass.ds(t + 2 * q, 2)].unsqueeze(2).to_broadcast((P, 2, P)),
                                    ALU.is_equal).then_inc(hot_made[q], 1)
                    dve.wait_ge(products_made[q], n1 * 2)
                    for j in (2 * q, 2 * q + 1):
                        for c in range(3):
                            comp = rows[:, h, j, 0:C3].rearrange("p (c k) -> p c k", k=3)[:, :, c]
                            v.scalar_tensor_tensor(out=comp, in0=rows[:, h, j, D:TW], scalar=ea_c[:, c, bass.ds(t + j, 1)],
                                                   in1=comp, op0=ALU.mult, op1=ALU.add).then_inc(msg_made[j], 1)
                dve.reg_add(turns, turns, 1)
                dve.reg_add(half_turns[h], half_turns[h], 1)
                dve.reg_mov(half, 1 - h)

            with dve.Fori(0, NW) as w:
                first, end = window_range(dve, w)
                in_half = dve.snap(half)
                for h in range(2):
                    with dve.If(in_half == h):
                        with dve.Fori(first, end, 2 * TJ) as t:
                            messages(w, t, h)
                            with dve.If(t + TJ < end):
                                messages(w, t + TJ, 1 - h)

            def take_counts(w):
                for c in range(3):
                    k0, k1 = 4 * c, min(NW, 4 * c + 4)
                    m = 3 * w + c
                    dve.wait_ge(S["counts_turned"], m + 1)
                    v.tensor_copy(countsT[:, k0:k1, w * P:(w + 1) * P],
                                  bank[6 + m % 2][:, 0:(k1 - k0) * P].rearrange("p (k f) -> p k f", f=P)
                                  ).then_inc(S["counts_taken"], 1)

            def difference(w):
                v.tensor_tensor(counts_f[:, 0:N], cumul[:, w, 1:NC1], cumul[:, w, 0:N], ALU.subtract).then_inc(S["counts_float"], 1)

            dve.wait_ge(S["counts_flushed"], NW + 1)
            dve.wait_ge(S["sums_flushed"], NW + 1)
            difference(0)
            for w in range(NW):
                b = w % 2
                dve.wait_ge(S["x1T_taken"], w + 1)
                v.tensor_copy(sT1[:, w * P:(w + 1) * P], x1T[:, b, C3:D]).then_inc(S["s1_taken"], 1)
                take_counts(w)
                if w + 1 < NW:
                    difference(w + 1)
                dve.wait_ge(S["v_squared"], w + 1)
                if w >= 2:
                    dve.wait_ge(S["norm_made"], w - 1)
                then(v.tensor_reduce(ssq[:, b, :], sq[:, :].rearrange("p (c k) -> p c k", k=3), AX.X, ALU.add))
                v.tensor_scalar(ssq[:, b, :], ssq[:, b, :], 2.0 ** -115, None, ALU.max).then_inc(S["norm_sq"], 1)
            for c, (lo, hi) in enumerate(THIRDS):
                dve.wait_ge(S["norm_turned"], min(NW, (c + 1) * 4))
                v.tensor_copy(nT[:, lo:hi], bank[5 + c][:, 0:hi - lo]).then_inc(S["norm_taken"], 1)
            for c, (lo, hi) in enumerate(THIRDS):
                dve.wait_ge(S["sig1_made"], c + 1)
                v.scalar_tensor_tensor(out=h1T[:, lo:hi], in0=bank[c][:, 0:hi - lo], scalar=bu1c[:, :], in1=h1T[:, lo:hi],
                                       op0=ALU.add, op1=ALU.mult).then_inc(S["h1_made"], 1)
            for w in range(NW):
                b = w % 2
                dve.wait_ge(S["gate_taken"], w + 1)
                dve.wait_ge(S["x_residual"], w + 1)
                vec = x1[:, w, 0:C3].rearrange("p (c k) -> p c k", k=3)
                v.tensor_tensor(vec, vu[:, w, :].rearrange("p (c k) -> p c k", k=3),
                                hh[:, b, 0:C].unsqueeze(2).to_broadcast((P, C, 3)), ALU.mult).then_inc(S["update_made"], 1)
                dve.wait_ge(S["update_made"], 2 * w + 1)
                then(v.tensor_tensor(prod[:, :], x1[:, w, 0:C3], vv[:, w, :], ALU.mult))
                then(v.tensor_reduce(dot, prod[:, :].rearrange("p (c k) -> p c k", k=3), AX.X, ALU.add))
                v.tensor_tensor(x1[:, w, C3:D], dot, hh[:, b, 2 * C:C3], ALU.add).then_inc(S["update_made"], 1)

            for w in range(NW):
                res, st = y[:, w % 2, :], stat[:, w, :]
                dve.wait_ge(S["window_done"], w + 1)
                v.tensor_tensor(res, xw[:, w, :], bank[out_bank(w)], ALU.add).then_inc(S["res_made"], 1)
                dve.wait_ge(S["res_made"], w + 1)
                v.bn_stats(st[:, 0:6], res).then_inc(S["ln_stats"], 1)
                dve.wait_ge(S["ln_stats"], w + 1)
                v.bn_aggr(st[:, 6:8], st[:, 0:6]).then_inc(S["ln_mean"], 1)
                dve.wait_ge(S["ln_mean"], w + 1)
                v.tensor_scalar(st[:, 8:9], st[:, 7:8], EPS, None, ALU.add).then_inc(S["var_made"], 1)
                dve.wait_ge(S["std_made"], w + 1)
                v.reciprocal(st[:, 10:11], st[:, 9:10]).then_inc(S["ln_scale"], 1)
                dve.wait_ge(S["ln_scale"], w + 1)
                v.tensor_scalar(xw[:, w, :], res, st[:, 6:7], st[:, 10:11], ALU.subtract, ALU.mult).then_inc(S["y_made"], 1)

        @block.tensor
        def _(pe):
            mm = nc.tensor.matmul
            turn_ = nc.tensor.transpose
            for j in range(TJ):
                pe.sem_inc(summed[j], 1)
            for b in range(2):
                pe.sem_inc(sign_used[b], 1)
            pe.wait_ge(S["pool_const"], 4)
            pe.wait_ge(S["edges_float"], 2)
            ea_k = ea_r.rearrange("g (e k) -> g e k", k=3)
            for i, a in enumerate((dst_f, src_f, ea_k[:, :, 0], ea_k[:, :, 1], ea_k[:, :, 2])):
                for j in range(TJ):
                    last = turn_(bank[i][:, j * GR:(j + 1) * GR], a[:, j * P:(j + 1) * P], ident[0:GR, 0:GR])
                last.then_inc(S["edges_turned"], 1)
            pe.wait_ge(S["span_made"], 2 * TJ)
            turn_(bank[5][0:TJ * 2 * W11, 0:GR], span[:, :, :, :].rearrange("p a b c -> p (a b c)"),
                  ident[0:GR, 0:GR]).then_inc(S["span_turned"], 1)
            pe.wait_ge(S["span_max"], 1)
            turn_(bank[5][0:1, 128:128 + TJ * 2 * W11], span_t[:, :],
                  ident[0:TJ * 2 * W11, 0:TJ * 2 * W11]).then_inc(S["span_row"], 1)
            pe.wait_ge(S["ld_x"], 32)
            pe.wait_ge(S["pads_set"], 6)
            pe.wait_ge(S["ranges_set"], 1)
            for c in range(3):
                for i in range(4 * c, min(NW, 4 * c + 4)):
                    last = turn_(bank[5 + c][:, (i % 4) * P:(i % 4 + 1) * P], xw[:, i, C3:D], ident[:, :])
                last.then_inc(S["s_turned"], 1)
            pe.wait_ge(S["ld_weights"], 16 * 10)
            for c, (lo, hi) in enumerate(THIRDS):
                pe.wait_ge(S["s_taken"], c + 1)
                mm(bank[5 + c][:, 0:hi - lo], w1[:, :], sT[:, lo:hi], start=True, stop=True).then_inc(S["z_made"], 1)
            pe.wait_ge(S["h_made"], 3)
            turn_(bank[6][:, 0:C], u_sb[:, :], ident[:, :]).then_inc(S["uv_turned"], 1)
            pe.wait_ge(S["uv_taken"], 1)
            mm(bank[7][:, 0:C], uT, v_sb[:, :], start=True, stop=True).then_inc(S["uv_made"], 1)
            pe.wait_ge(S["edges_taken"], 6)
            pe.wait_ge(S["picks_made"], 2)
            pe.wait_ge(S["uv_set"], 1)

            def spread(i):
                pe.wait_ge(rc_loaded, 32 * (i + 1))
                for k in range(2):
                    if i:
                        pe.wait_ge(S[("turn_made", "wave_scaled")[k]], i)
                    for b in range(PB):
                        last = mm(psum[0:RROWS, k * PB + b, 0:PW], pick[:, k].rearrange("p n c -> p (n c)"),
                                  rc_piece[:, k, b * PW:(b + 1) * PW], start=True, stop=True)
                    last.then_inc(S["rc_spread"], 1)

            def filter_of(w):
                if w >= 2:
                    pe.wait_ge(S["table_rest_made"], w - 1)
                mm(bank[6 + w % 2][:, 0:C3], hT[:, w * P:(w + 1) * P], w3[:, :], start=True, stop=False)
                mm(bank[6 + w % 2][:, 0:C3], ones_row[:, :], b3r[:, :], start=False, stop=True).then_inc(S["filter_made"], 1)

            spread(0)
            for i in range(PIECES):
                for w in (2 * i, 2 * i + 1):
                    if w < NW:
                        filter_of(w)
                if i + 1 < PIECES:
                    spread(i + 1)

            def basis(t, q):
                if q == 0:
                    last = pe.snap(t + (TJ - 1 + PIECE_TILES))
                    pe.reg_alu(pieces, pe.snap(last * RECIP), 16, ALU.logical_shift_right)
                    pe.reg_alu(pieces_had, pieces, PIECES, ALU.min)
                    pe.reg_alu(pieces_awaited, pieces_had, 1, ALU.max)
                    pe.reg_alu(moved, pieces_awaited, 16 * PARTS, ALU.mult)
                    pe.wait_ge(S["parts_moved"], moved)
                for j in (2 * q, 2 * q + 1):
                    last = mm(bank[j][:, 0:C3], radial[0:RROWS + 3, bass.ds((t + j) * P, P)], w2s[:, :], start=True, stop=True)
                last.then_inc(basis_made[q], 1)

            PIECE_TILES = PC // P
            RECIP = (1 << 16) // PIECE_TILES + 1
            assert all(n * RECIP >> 16 == n // PIECE_TILES for n in range(NT + 2 * TJ + PIECE_TILES))
            pieces, pieces_had, pieces_awaited, moved = [
                pe.alloc_register(n) for n in ("pieces_needed", "pieces_to_have", "pieces_awaited", "pieces_moved")]
            pe.wait_ge(S["w2_moved"], 16 * (PARTS + 3))
            pe.wait_ge(S["table_rest_made"], NW)
            pe.wait_ge(S["wave_scaled"], PIECES)
            turns = pe.alloc_register("summed_group_turn")
            over = pe.alloc_register("past_the_window")
            pe.reg_mov(turns, 1)
            half = pe.alloc_register("half_to_sum")
            pe.reg_mov(half, 0)
            t0 = pe.value_load(rng[0:1, 0:1], min_val=0, max_val=NT - 1)
            for q in range(2):
                basis(t0, q)

            def sums(t, end, first_next, h):
                n1 = pe.snap(turns)
                pe.reg_alu(over, t + TJ, end, ALU.is_ge)
                o = pe.snap(over)
                nxt = pe.snap(t + TJ + o * (first_next - t - TJ), min_val=0, max_val=NT - 1)
                for q in range(2):
                    pe.wait_ge(hot_made[q], n1)
                    for j in (2 * q, 2 * q + 1):
                        pe.wait_ge(sign_made[j % 2], 2 * n1 - 1 + j // 2)
                        for b in range(3):
                            last = mm(bank[5 + b][:, 0:CB], onehot_bf[:, j, :], sign[:, j % 2, b * CB:(b + 1) * CB],
                                      start=False, stop=True, skip_group_check=True)
                        last.then_inc(sign_used[j % 2], 1)
                    pe.wait_ge(products_made[q], n1 * 2)
                    basis(nxt, q)
                    pe.wait_ge(hot_widened[q], n1)
                    for j in (2 * q, 2 * q + 1):
                        pe.wait_ge(msg_made[j], n1 * 3)
                        mm(bank[4], onehot[:, j, :], rows[:, bass.ds(h, 1), j, 0:D].rearrange("p h f -> p (h f)"), start=False, stop=True,
                           skip_group_check=True).then_inc(summed[j], 1)
                pe.reg_add(turns, turns, 1)

            with pe.Fori(0, NW) as w:
                first, end = window_range(pe, w)
                first_next = pe.value_load(rng[0:1, bass.ds(w + 1, 1)], min_val=0, max_val=NT - 1)
                pe.wait_ge(S["counts_flushed"], w + 1)
                for b in range(3):
                    mm(bank[5 + b][:, 0:CB], zeros_bf[:, 0:P], zeros_bf[:, 0:CB], start=True, stop=True, skip_group_check=True)
                pe.wait_ge(S["sums_flushed"], w + 1)
                mm(bank[4], zeros_bf[:, 0:P], zeros_bf[:, :], start=True, stop=True, skip_group_check=True)
                with pe.Fori(first, end, TJ) as t:
                    sums(t, end, first_next, pe.snap(half, min_val=0, max_val=1))
                    pe.reg_alu(half, 1, half, ALU.subtract)
                mm(bank[4], zeros_bf[:, 0:P], zeros_bf[:, :], start=False, stop=True, skip_group_check=True
                   ).then_inc(S["window_summed"], 1)

            for w in range(NW):
                b = w % 2
                pe.wait_ge(S["node_added"], w + 1)
                if w >= 2:
                    pe.wait_ge(S["x1T_taken"], w - 1)
                for i in range(4):
                    last = turn_(bank[b][:, i * P:(i + 1) * P], x1[:, w, i * P:(i + 1) * P], ident[:, :])
                last.then_inc(S["x1T_turned"], 1)
                pe.wait_ge(S["counts_float"], w + 2)
                for c in range(3):
                    m = 3 * w + c
                    if m >= 2:
                        pe.wait_ge(S["counts_taken"], m - 1)
                    for k in range(4 * c, min(NW, 4 * c + 4)):
                        last = turn_(bank[6 + m % 2][:, (k % 4) * P:(k % 4 + 1) * P], counts_f[:, k * P:(k + 1) * P], ident[:, :])
                    last.then_inc(S["counts_turned"], 1)
                pe.wait_ge(S["x1T_taken"], w + 1)
                if w >= 2:
                    pe.wait_ge(S["v_squared"], w - 1)
                for i in range(3):
                    lhs = x1T[:, b, i * C:(i + 1) * C]
                    mm(bank[2 + b][:, i * C:(i + 1) * C], lhs, u_sb[:, :], start=True, stop=True)
                    last = mm(bank[4 + b][:, i * C:(i + 1) * C], lhs, uv_sb[:, :], start=True, stop=True)
                last.then_inc(S["v_made"], 1)
            pe.wait_ge(S["v_squared"], NW)
            pe.wait_ge(S["counts_taken"], 3 * NW)
            for w in range(NW):
                pe.wait_ge(S["norm_made"], w + 1)
                turn_(bank[5 + w // 4][:, (w % 4) * P:(w % 4 + 1) * P], nrm[:, w, :], ident[:, :]).then_inc(S["norm_turned"], 1)
            pe.wait_ge(S["s1_taken"], NW)
            for c, (lo, hi) in enumerate(THIRDS):
                pe.wait_ge(S["norm_taken"], c + 1)
                mm(bank[c][:, 0:hi - lo], wu1[:, 0, :], nT[:, lo:hi], start=True, stop=False)
                mm(bank[c][:, 0:hi - lo], wu1[:, 1, :], sT1[:, lo:hi], start=False, stop=True).then_inc(S["z1_made"], 1)

            def second_messages(d, s):
                n = P if s < NFULL else NTAIL
                return mm(bank[out_bank(d)], countsT[0:n, s, d * P:(d + 1) * P], x1[0:n, s, :],
                          start=(s == 0), stop=(s == NW - 1))

            pe.wait_ge(S["norm_taken"], 3)
            for w in range(NW + 1):
                if w < NW:
                    pe.wait_ge(S["h1_made"], w // 4 + 1)
                    if w >= 2:
                        pe.wait_ge(S["gate_taken"], w - 1)
                    mm(bank[3 + w % 2][:, 0:C3], h1T[:, w * P:(w + 1) * P], wu2[:, :], start=True, stop=False)
                    mm(bank[3 + w % 2][:, 0:C3], ones_row[:, :], bu2r[:, :], start=False, stop=True).then_inc(S["gate_made"], 1)
                if w:
                    pe.wait_ge(S["update_made"], 2 * w)
                    for d in range(EARLY):
                        last = second_messages(d, w - 1)
                        if w == NW:
                            last.then_inc(S["window_done"], 1)
            pe.wait_ge(S["gate_taken"], NW)
            for d in range(EARLY, NW):
                if d >= EARLY + 4:
                    pe.wait_ge(S["res_made"], d - 3)
                for s in range(NW):
                    last = second_messages(d, s)
                last.then_inc(S["window_done"], 1)


_INS = ['x', 'src', 'dst', 'edge_attr_3', 'edge_weight', 'L0_gnn_W1', 'L0_gnn_b1', 'L0_gnn_W2', 'L0_gnn_b2',
        'L0_gnn_W3', 'L0_gnn_b3', 'L0_gnn_U', 'L0_gnn_V', 'L0_gnn_Wu1', 'L0_gnn_bu1', 'L0_gnn_Wu2', 'L0_gnn_bu2']


def kernel(**inputs):
    import concourse.bacc as bacc
    from concourse.bass_utils import run_bass_kernel_spmd

    nc = bacc.Bacc("TRN2", target_bir_lowering=False, num_devices=1)
    arrays, args = {}, []
    for name in _INS:
        a = np.ascontiguousarray(inputs[name])
        arrays[f"in_{name}"] = a
        args.append(nc.dram_tensor(f"in_{name}", a.shape, mybir.dt.from_np(a.dtype), kind="ExternalInput").ap())
    out = nc.dram_tensor("out", inputs["x"].shape, F32, kind="ExternalOutput").ap()
    build(nc, *args, out)
    r = run_bass_kernel_spmd(nc, [arrays], core_ids=[0])
    return r.results[0]["out"]
```

```python
from contextlib import ExitStack

import concourse.bass as bass
from concourse import mybir
import numpy as np

F32 = mybir.dt.float32
BF16 = mybir.dt.bfloat16
I32 = mybir.dt.int32
U16 = mybir.dt.uint16
F16 = mybir.dt.float16
ALU = mybir.AluOpType
ACT = mybir.ActivationFunctionType
AX = mybir.AxisListType

P = 128
R_CUT = 1.4415
N_RBF = 20
EPS = 1e-5
MAGIC = 1.5 * 2.0 ** 23
TWO_ONES = float(np.array([0x3F803F80], np.uint32).view(np.float32)[0])
TWO_PI = float(np.nextafter(np.float32(2 * np.pi), np.float32(0)))
TJ = 4
GE = TJ * P
PARTS = 6
STACK = (0, 0, 0, 1, 1, 2)
STACK_W = (0, 1, 2, 0, 1, 0)
CHUNKS = 6
PIECES = 6
PB = 3


def build(nc, x, src, dst, ea, ew, W1, b1, W2, b2, W3, b3, U, V, Wu1, bu1, Wu2, bu2, out):
    N, D = x.shape
    E = src.shape[0]
    C = W1.shape[0]
    C3 = 3 * C
    TW = C3 + 2 * C
    NW = -(-N // P)
    NFULL = N // P
    NTAIL = N - NFULL * P
    NT = -(-E // P)
    NGF = E // GE
    ETAIL = E - NGF * GE
    GR = 81
    NPAD = NW * P
    RROWS = CHUNKS * N_RBF
    CH = GR * GE // CHUNKS
    PC = CH // PIECES
    PW = PC // PB
    GW = CHUNKS * CH
    NC1 = N + 1
    CB = NC1 // 3
    W11 = NW + 1
    PACK_BITS = 9
    PACK = 1 << PACK_BITS
    assert NT < PACK
    assert CHUNKS * PIECES * PB * PW == GR * GE and (NT + TJ - 1) * P <= GW and C == P and 3 * CB == NC1
    assert PARTS * N_RBF == RROWS

    node_table = nc.dram_tensor("node_table", (NPAD, TW), F32, kind="Internal").ap()
    rc_rows = nc.dram_tensor("rc_rows", (2, 3, GR * GE), BF16, kind="Internal").ap()
    part_rows = nc.dram_tensor("part_rows", (3, RROWS, CH), BF16, kind="Internal").ap()

    with ExitStack() as ctx:
        def sb(name, shape, dt=F32):
            return ctx.enter_context(nc.sbuf_tensor(name, shape, dt))

        def sem(name):
            return ctx.enter_context(nc.semaphore(name))

        psum = ctx.enter_context(nc.psum_tensor("psum", [P, 8, 512], F32))
        bank = [psum[:, i, :] for i in range(8)]

        class Region:

            def __init__(self, ap, width):
                self.ap, self.width, self.at = ap, width, 0

            def cut(self, width, dt=F32, rows=P):
                words = width if dt in (F32, I32) else -(-width // 2)
                a = self.ap[0:rows, self.at:self.at + words]
                self.at += words
                assert self.at <= self.width
                if dt in (BF16, F16, U16):
                    return a.bitcast(dt)[:, 0:width]
                return a if dt == F32 else a.bitcast(dt)

        radial = sb("radial", [P, GW], BF16)
        work = sb("work", [P, NW * D + 2 * TJ * TW])
        side = sb("side", [P, 9328])

        def regions():
            return (Region(radial[:, :].bitcast(F32), GW // 2), Region(work, NW * D + 2 * TJ * TW), Region(side, 9328))

        ident = sb("ident", [P, P])
        node_no = sb("node_no", [P, NPAD + 2], F16)
        ones_bf = sb("ones_bf", [3, P], BF16)
        zeros_bf = sb("zeros_bf", [P, 512], BF16)
        w1 = sb("w1", [P, C])
        w3 = sb("w3", [P, C3])
        u_sb = sb("u_sb", [P, C])
        v_sb = sb("v_sb", [P, C])
        uv_sb = sb("uv_sb", [P, C])
        wu1 = sb("wu1", [P, 2, C])
        wu2 = sb("wu2", [P, C3])
        b1c = sb("b1c", [P, 1])
        bu1c = sb("bu1c", [P, 1])
        bias_parts = sb("bias_parts", [3, 2 * C3], BF16)
        w2s = sb("w2s", [RROWS + 3, C3], BF16)
        pick = sb("pick", [3 * CHUNKS, N_RBF, CHUNKS], BF16)
        harmonic = sb("harmonic", [RROWS, 1])
        half_pi = sb("half_pi", [GR, 1])
        count_bias = sb("count_bias", [P, 1])

        xw = sb("xw", [P, NW, D])
        dst_c = sb("dst_c", [P, GR * TJ], F16)
        src_c = sb("src_c", [P, GR * TJ], I32)
        src_b = sb("src_b", [P, GR * TJ])
        ea_c = sb("ea_c", [P, 3, GR * TJ])
        idx = sb("idx", [P, 2, TJ], I32)
        onehot = sb("onehot", [P, TJ, P])
        sign = sb("sign", [P, 2, NC1 + 1], BF16)
        onehot_bf = sb("onehot_bf", [P, TJ, P], BF16)
        rng = sb("rng", [1, W11], I32)

        r_rad, r_work, r_side = regions()
        w2f = r_rad.cut(C3, rows=N_RBF)
        bf = r_rad.cut(3 * C3, rows=1)
        w2p = r_rad.cut(3 * C3, BF16, rows=N_RBF).rearrange("p (k f) -> p k f", k=3)
        bp = r_rad.cut(9 * C3, BF16, rows=1).rearrange("p (k f) -> p k f", k=3)
        rc_parts = r_rad.cut(6 * GE, BF16, rows=GR).rearrange("p (k q f) -> p k q f", k=2, q=3)
        r_left = r_rad.cut(GE, rows=GR)
        node_no_i = r_rad.cut(NPAD + 2, I32)
        pick_i = r_rad.cut(RROWS, I32, rows=3 * CHUNKS).rearrange("p (n c) -> p n c", n=N_RBF)
        pick_f = r_rad.cut(RROWS, rows=3 * CHUNKS).rearrange("p (n c) -> p n c", n=N_RBF)
        row_i = r_rad.cut(1, I32, rows=RROWS)
        src_i = r_work.cut(GE, I32, rows=GR)
        dst_i = r_work.cut(GE, I32, rows=GR)
        dst_hi_i = r_work.cut(GE, I32, rows=GR)
        ea_r = r_work.cut(3 * GE, rows=GR)
        r_r = r_work.cut(GE, rows=GR)
        src_f = r_work.cut(GE, rows=GR)
        dst_f = r_work.cut(GE, rows=GR)
        coef = r_work.cut(GE, rows=GR)
        tmp_a = r_work.cut(GE, rows=GR)
        tmp_b = r_work.cut(GE, rows=GR)
        sT = r_work.cut(NPAD)
        hT = r_work.cut(NPAD)
        table_out = r_work.cut(2 * TW).rearrange("p (b f) -> p b f", b=2)
        turn = r_side.cut(PC, rows=RROWS).rearrange("p (b f) -> p b f", b=PB)
        wave = r_side.cut(2 * PC, rows=RROWS).rearrange("p (d f) -> p d f", d=2)
        part = r_side.cut(6 * PC, BF16, rows=RROWS).rearrange("p (d k f) -> p d k f", d=2, k=3)
        rc_piece = r_side.cut(2 * PC, BF16, rows=3 * CHUNKS).rearrange("p (k f) -> p k f", k=2)
        nearest = r_side.cut(PC, rows=RROWS)
        first_filter = onehot[:, 0:2, :]
        uT = sT[:, 0:C]
        tile_no_i = r_work.cut(TJ, I32, rows=GR)
        tile_no = r_work.cut(TJ, rows=GR)
        win_lo_i = r_work.cut(W11, I32, rows=GR)
        win_lo = r_work.cut(W11, rows=GR)
        least = r_work.cut(TJ, rows=GR)
        most = r_work.cut(TJ, rows=GR)
        to_last = r_work.cut(TJ, rows=GR)
        past = r_work.cut(TJ, rows=GR)
        in_span = r_work.cut(W11, rows=GR)
        span = r_work.cut(TJ * 2 * W11, rows=GR).rearrange("p (j k w) -> p j k w", j=TJ, k=2)
        rng_f = r_work.cut(2 * W11, rows=1).rearrange("p (k w) -> p k w", k=2)
        span_t = r_work.cut(1, rows=TJ * 2 * W11)

        r_rad, r_work, r_side = regions()
        x1 = r_work.cut(NW * D).rearrange("p (w f) -> p w f", w=NW)
        rows = r_work.cut(2 * TJ * TW).rearrange("p (h j f) -> p h j f", h=2, j=TJ)
        cumul = r_side.cut(NW * (NC1 + 1), U16).rearrange("p (w f) -> p w f", w=NW)

        r_rad, r_work, r_side = regions()
        countsT = r_rad.cut(2 * NW * NPAD, BF16).rearrange("p (r s d) -> p r s d", r=2, s=NW)
        vuv = r_rad.cut(2 * NW * C3)
        vu = vuv.rearrange("p (w k f) -> p w k f", w=NW, k=2)[:, :, 0, :]
        vv = vuv.rearrange("p (w k f) -> p w k f", w=NW, k=2)[:, :, 1, :]
        update_parts = vuv.bitcast(BF16).rearrange("p (w k f) -> p w k f", w=NW, k=3)
        ident_bf = r_rad.cut(P, BF16)
        degree = r_rad.cut(NW)
        most_edges = r_rad.cut(1)
        many_f = r_rad.cut(1, rows=1)
        many = r_rad.cut(1, I32, rows=1)
        r_work.cut(NW * D)
        x1T = r_work.cut(2 * D).rearrange("p (b f) -> p b f", b=2)
        sT1 = r_work.cut(NPAD)
        nrm = r_work.cut(NPAD).rearrange("p (w f) -> p w f", w=NW)
        nT = r_work.cut(NPAD)
        r_side.cut(NW * (NC1 + 1), U16)
        h1T = r_side.cut(NPAD)
        counts_b = r_side.cut(NPAD, BF16)
        rest_b = r_side.cut(NPAD, BF16)
        counts_f = h1T[:, 0:N]
        sq = r_side.cut(C3)
        stat = r_side.cut(NW * 12).rearrange("p (w f) -> p w f", w=NW)
        ssq = r_work.cut(2 * C).rearrange("p (b f) -> p b f", b=2)
        prod, dot = sq, ssq[:, 0, :]
        y = x1T
        hh = x1T[:, :, 0:C3]

        names = """ld_x ld_r ld_edges ld_w2 ld_weights pads_set pool_const picks_made dve_const half_pi_set dve_step cos_in
        cos_done rc_made r_split coef_split rc_stored turns_taken turn_made sin_done wave_scaled hi_made wave_less_hi
        mid_made lo_made parts_moved w2_split w2_moved edges_float edges_turned edges_taken span_made span_turned
        span_max span_row ranges_set s_turned s_taken z_made sig_made h_made filter_made filter_taken table_vec_made
        table_rest_made uv_turned uv_taken uv_made uv_set window_summed sums_flushed counts_flushed node_added
        x1T_turned x1T_taken v_made v_taken v_squared norm_sq norm_made norm_turned norm_taken s1_taken z1_made
        sig1_made h1_made gate_made gate_taken update_made counts_made counts_turned counts_copied counts_taken
        stage3_const most_made most_turned many_set rest_step rest_made rest_turned rest_taken update_hi update_less_hi
        update_mid update_split window_done res_made ln_stats ln_mean var_made std_made ln_scale y_made y_stored
        x_residual""".split()
        S = {n: sem(n) for n in names}
        rc_loaded = [sem(f"rc_loaded{k}") for k in range(2)]
        rc_spread = [sem(f"rc_spread{k}") for k in range(2)]
        parts_stored = [sem(f"parts_stored{b}") for b in range(2)]
        table_stored = [sem(f"table_stored{b}") for b in range(2)]
        gathered = [[sem(f"gathered{h}_{j}") for j in range(TJ)] for h in range(2)]
        indices_set = [[sem(f"indices_set{h}_{q}") for q in range(2)] for h in range(2)]
        products_made = [sem(f"products_made{q}") for q in range(2)]
        basis_made = [sem(f"basis_made{q}") for q in range(2)]
        hot_made = [sem(f"hot_made{q}") for q in range(2)]
        hot_widened = [sem(f"hot_widened{q}") for q in range(2)]
        msg_made = [sem(f"msg_made{j}") for j in range(TJ)]
        summed = [sem(f"summed{j}") for j in range(TJ)]
        sign_made = [sem(f"sign_made{b}") for b in range(2)]
        sign_used = [sem(f"sign_used{b}") for b in range(2)]
        THIRDS = ((0, 512), (512, 1024), (1024, NPAD))

        EARLY = 3

        def out_bank(w):
            return 5 + w if w < EARLY else (w - EARLY) % 4

        def through(n, b):
            return (n + 1 - b) // 2

        def window_range(eng, w, regs):
            packed = eng.value_load(rng[0:1, bass.ds(w, 1)], min_val=PACK, max_val=PACK * NT + NT - 1)
            eng.reg_alu(regs[1], packed, PACK_BITS, ALU.logical_shift_right)
            eng.reg_alu(regs[0], regs[1], PACK, ALU.mult)
            eng.reg_alu(regs[0], packed, regs[0], ALU.subtract)
            return eng.snap(regs[0], min_val=0, max_val=NT - 1), eng.snap(regs[1], min_val=1, max_val=NT)

        block = ctx.enter_context(nc.Block())

        @block.sync
        def _(sp):
            def load_rows(a, b_, width, done):
                sp.dma_start(a[0:NGF, :], b_[0:NGF * GE * width].rearrange("(g f) -> g f", f=GE * width)).then_inc(done, 16)
                sp.dma_start(a[NGF:NGF + 1, 0:ETAIL * width],
                             b_[NGF * GE * width:E * width].rearrange("(g f) -> g f", g=1)).then_inc(done, 16)

            sp.dma_start(w2f, W2).then_inc(S["ld_w2"], 16)
            sp.wait_ge(S["pads_set"], 1)
            load_rows(r_r, ew, 1, S["ld_r"])
            for i, b_ in enumerate((b2, b3, bu2)):
                sp.dma_start(bf[:, i * C3:(i + 1) * C3], b_.rearrange("(a f) -> a f", a=1)).then_inc(S["ld_w2"], 16)
            sp.wait_ge(S["pads_set"], 6)
            for a, b_, width in ((dst_i, dst, 1), (dst_hi_i, dst, 1), (src_i, src, 1), (ea_r, ea.rearrange("e k -> (e k)"), 3)):
                load_rows(a, b_, width, S["ld_edges"])
            sp.dma_start(xw[:, 0:NFULL, :], x[0:NFULL * P, :].rearrange("(w p) f -> p w f", p=P)).then_inc(S["ld_x"], 16)
            sp.dma_start(xw[0:NTAIL, NFULL, :], x[NFULL * P:N, :]).then_inc(S["ld_x"], 16)
            for a, b_ in ((w1[:, :], W1), (w3[:, :], W3), (b1c[:, :], b1.rearrange("(p a) -> p a", a=1)),
                          (u_sb[:, :], U), (v_sb[:, :], V),
                          (wu1[:, :, :], Wu1.rearrange("(k p) f -> p k f", p=P)),
                          (bu1c[:, :], bu1.rearrange("(p a) -> p a", a=1)), (wu2[:, :], Wu2)):
                sp.dma_start(a, b_).then_inc(S["ld_weights"], 16)
            for k, split in enumerate(("r_split", "coef_split")):
                sp.wait_ge(S[split], (4, 1)[k])
                sp.dma_start(rc_rows[k].rearrange("q (g f) -> g q f", f=GE), rc_parts[:, k]).then_inc(S["rc_stored"], 16)
            sp.wait_ge(S["w2_split"], 2)
            for q, k in enumerate(STACK_W):
                sp.dma_start(w2s[q * N_RBF:(q + 1) * N_RBF, :], w2p[:, k, :]).then_inc(S["w2_moved"], 16)
            for k in range(3):
                sp.dma_start(w2s[RROWS + k:RROWS + k + 1, :], bp[:, k, 0:C3]).then_inc(S["w2_moved"], 16)
                sp.dma_start(bias_parts[k:k + 1, :], bp[:, k, C3:3 * C3]).then_inc(S["w2_moved"], 16)
            AHEAD = PIECES // 3

            def load_stack(i):
                sp.wait_ge(parts_stored[i % 2], 16 * (i // 2 + 1))
                if i:
                    sp.wait_ge(S["parts_moved"], 16 * PARTS * i)
                else:
                    sp.wait_ge(S["pads_set"], 7)
                for q, k in enumerate(STACK):
                    sp.dma_start(radial[q * N_RBF:(q + 1) * N_RBF, :].rearrange("p (c f) -> p c f", c=CHUNKS)[:, :, i * PC:(i + 1) * PC],
                                 part_rows[k].rearrange("(n c) f -> n c f", c=CHUNKS)[:, :, i * PC:(i + 1) * PC]
                                 ).then_inc(S["parts_moved"], 16)

            for i in range(PIECES):
                sp.wait_ge(S["lo_made"], i + 1)
                sp.dma_start(part_rows[:, :, i * PC:(i + 1) * PC].rearrange("k p f -> p k f"), part[:, i % 2, :, :]
                             ).then_inc(parts_stored[i % 2], 16)
                if 1 <= i <= AHEAD:
                    load_stack(i - 1)
            sp.wait_ge(gathered[0][1], 16)
            for i in range(AHEAD, PIECES):
                load_stack(i)
            for w in range(NW):
                n = P if w < NFULL else NTAIL
                sp.wait_ge(S["y_made"], w + 1)
                sp.dma_start(out[w * P:w * P + n, :], xw[0:n, w, :]).then_inc(S["y_stored"], 16)
            sp.wait_ge(S["y_stored"], 16 * NW)

        @block.gpsimd
        def _(pool):
            g = nc.gpsimd
            g.memset(r_r, 1.0).then_inc(S["pads_set"], 1)
            g.memset(dst_i, -1).then_inc(S["pads_set"], 1)
            g.memset(dst_hi_i, 2 * NPAD).then_inc(S["pads_set"], 1)
            g.memset(src_i, 0).then_inc(S["pads_set"], 1)
            g.memset(ea_r, 0.0).then_inc(S["pads_set"], 1)
            g.memset(xw[:, NFULL, :], 0.0).then_inc(S["pads_set"], 1)
            pool.wait_ge(S["ld_r"], 32)
            g.tensor_copy(rc_parts[:, 0, 0], r_r).then_inc(S["r_split"], 1)
            pool.wait_ge(S["r_split"], 1)
            g.tensor_tensor(r_left, r_r, rc_parts[:, 0, 0], ALU.subtract).then_inc(S["r_split"], 1)
            pool.wait_ge(S["r_split"], 2)
            g.tensor_copy(rc_parts[:, 0, 1], r_left).then_inc(S["r_split"], 1)
            pool.wait_ge(S["r_split"], 3)
            g.tensor_tensor(rc_parts[:, 0, 2], r_left, rc_parts[:, 0, 1], ALU.subtract).then_inc(S["r_split"], 1)
            g.iota(row_i, pattern=[[0, 1]], base=0, channel_multiplier=1).then_inc(S["pool_const"], 1)
            g.iota(pick_i, pattern=[[0, N_RBF], [1, CHUNKS]], base=0, channel_multiplier=-1).then_inc(S["pool_const"], 1)
            g.memset(ident[:, :], 0.0).then_inc(S["pool_const"], 1)
            pool.wait_ge(S["pool_const"], 3)
            g.affine_select(out=ident[:, :], in_=ident[:, :], compare_op=ALU.not_equal, fill=1.0, base=0,
                            pattern=[[-1, P]], channel_multiplier=1).then_inc(S["pool_const"], 1)
            g.iota(tile_no_i[:, :], pattern=[[1, TJ]], base=0, channel_multiplier=TJ).then_inc(S["pool_const"], 1)
            g.iota(win_lo_i[:, :], pattern=[[P, W11]], base=0, channel_multiplier=0).then_inc(S["pool_const"], 1)
            g.iota(node_no_i, pattern=[[1, NPAD + 2]], base=-2, channel_multiplier=0).then_inc(S["pool_const"], 1)
            pool.wait_ge(S["dve_const"], 3)
            pool.wait_ge(S["picks_made"], 2)
            pool.wait_ge(S["w2_moved"], 16 * (PARTS + 6))
            pool.wait_ge(S["rc_stored"], 32)
            g.memset(radial[96:P, :].bitcast(F32), TWO_ONES).then_inc(S["pads_set"], 1)
            pool.wait_ge(S["pads_set"], 7)
            for i in range(PIECES - 1):
                b = i % 2
                pool.wait_ge(S["hi_made"], i + 1)
                g.tensor_tensor(wave[:, b, :], wave[:, b, :], part[:, b, 0, :], ALU.subtract).then_inc(S["wave_less_hi"], 1)
                pool.wait_ge(S["mid_made"], i + 1)
                g.tensor_tensor(part[:, b, 2, :], wave[:, b, :], part[:, b, 1, :], ALU.subtract).then_inc(S["lo_made"], 1)

            after = [pool.alloc_register(f"turn_of_pair{q}_after") for q in range(2)]
            slot_turns = [[pool.alloc_register(f"turns_of_slot{h}_{q}") for q in range(2)] for h in range(2)]
            slot_free = [[pool.alloc_register(f"slot{h}_{q}_is_free") for q in range(2)] for h in range(2)]
            half = pool.alloc_register("half_to_gather_to")
            pool.reg_mov(half, 0)
            for q in range(2):
                pool.reg_mov(after[q], 2)
                for h in range(2):
                    pool.reg_mov(slot_turns[h][q], 1)
                    pool.reg_mov(slot_free[h][q], 1)
            pool.wait_ge(S["ranges_set"], 1)
            pool.wait_ge(S["edges_taken"], 6)
            for b in range(2):
                pool.wait_ge(table_stored[b], 16 * through(NW, b))

            def gathers(t, h, q):
                turn = pool.snap(slot_turns[h][q])
                free = pool.snap(slot_free[h][q])
                at = pool.snap(t, min_val=0, max_val=NT + TJ - 1)
                pool.wait_ge(S["ranges_set"], 1)
                pool.wait_ge(summed[2 * q], free)
                pool.wait_ge(summed[2 * q + 1], free)
                g.tensor_copy(idx[:, h, 2 * q:2 * q + 2], src_c[:, bass.ds(at + 2 * q, 2)]).then_inc(indices_set[h][q], 1)
                for j in (2 * q, 2 * q + 1):
                    pool.wait_ge(S["ranges_set"], 1)
                    if j == 2 * q:
                        pool.wait_ge(indices_set[h][q], turn)
                    g.indirect_dma_start(
                        out=rows[:, h, j, :], out_offset=None, in_=node_table,
                        in_offset=bass.IndirectOffsetOnAxis(ap=idx[:, h, j:j + 1], axis=0)).then_inc(gathered[h][j], 16)
                pool.reg_add(slot_turns[h][q], slot_turns[h][q], 1)
                pool.reg_mov(slot_free[h][q], after[q])
                pool.reg_add(after[q], after[q], 1)

            def group_gathers(t, end, h):
                gathers(t, h, 0)
                with pool.If(t + 2 < end):
                    gathers(t, h, 1)
                pool.reg_mov(half, 1 - h)

            window_regs = [pool.alloc_register(n) for n in ("first_tile", "end_tile")]
            with pool.Fori(0, NW) as w:
                first, end = window_range(pool, w, window_regs)
                in_half = pool.snap(half)
                for h in range(2):
                    with pool.If(in_half == h):
                        with pool.Fori(first, end, 2 * TJ) as t:
                            group_gathers(t, end, h)
                            with pool.If(t + TJ < end):
                                group_gathers(t + TJ, end, 1 - h)
            pool.wait_ge(S["counts_flushed"], NW + 1)
            pool.wait_ge(S["sums_flushed"], NW + 1)
            g.memset(counts_b[:, N:NPAD], 0.0).then_inc(S["stage3_const"], 1)
            g.memset(rest_b[:, N:NPAD], 0.0).then_inc(S["stage3_const"], 1)
            g.tensor_copy(ident_bf, ident[:, :]).then_inc(S["stage3_const"], 1)
            for w in range(NW):
                g.tensor_tensor(x1[:, w, :], x1[:, w, :], xw[:, w, :], ALU.add).then_inc(S["node_added"], 1)
                pool.wait_ge(S["node_added"], w + 1)
                g.tensor_tensor(xw[:, w, :], xw[:, w, :], x1[:, w, :], ALU.add).then_inc(S["x_residual"], 1)
            for w in range(NW):
                pool.wait_ge(S["update_hi"], w + 1)
                g.tensor_tensor(x1[:, w, :], x1[:, w, :], update_parts[:, w, 0, :], ALU.subtract).then_inc(S["update_less_hi"], 1)
                pool.wait_ge(S["update_mid"], w + 1)
                g.tensor_tensor(update_parts[:, w, 2, :], x1[:, w, :], update_parts[:, w, 1, :], ALU.subtract
                                ).then_inc(S["update_split"], 1)

        @block.scalar
        def _(act):
            a = nc.scalar
            act.sem_inc(S["sums_flushed"], 1)
            act.sem_inc(S["counts_flushed"], 1)
            act.wait_ge(S["cos_in"], 1)
            act.wait_ge(S["half_pi_set"], 1)
            a.activation(tmp_b, tmp_a, ACT.Sin, bias=half_pi[:, :], scale=-float(np.pi / R_CUT)).then_inc(S["cos_done"], 1)

            def load_piece(i, k):
                if i:
                    act.wait_ge(rc_spread[k], i)
                a.dma_start(rc_piece[:, k, :], rc_rows[k, :, 0:GW].rearrange("q (c f) -> (q c) f", c=CHUNKS)
                            [:, i * PC:(i + 1) * PC]).then_inc(rc_loaded[k], 16)

            act.wait_ge(S["rc_stored"], 32)
            for k in range(2):
                load_piece(0, k)
            for c, (lo, hi) in enumerate(THIRDS):
                act.wait_ge(S["z_made"], c + 1)
                a.activation(hT[:, lo:hi], bank[5 + c][:, 0:hi - lo], ACT.Sigmoid, bias=b1c[:, :]).then_inc(S["sig_made"], 1)

            def take_filter(w):
                b = w % 2
                act.wait_ge(S["filter_made"], w + 1)
                if w >= 2:
                    act.wait_ge(table_stored[b], 16 * (w // 2))
                    act.wait_ge(S["table_vec_made"], w - 1)
                a.copy(first_filter[:, b, :], bank[6 + b][:, 0:C]).then_inc(S["filter_taken"], 1)
                a.copy(table_out[:, b, C3:TW], bank[6 + b][:, C:C3]).then_inc(S["table_rest_made"], 1)

            def store_table(w):
                act.wait_ge(S["table_vec_made"], w + 1)
                act.wait_ge(S["table_rest_made"], w + 1)
                a.dma_start(node_table[w * P:(w + 1) * P, :], table_out[:, w % 2, :]).then_inc(table_stored[w % 2], 16)

            def middle(i):
                act.wait_ge(S["wave_less_hi"], i + 1)
                a.copy(part[:, i % 2, 1, :], wave[:, i % 2, :]).then_inc(S["mid_made"], 1)

            for i in range(PIECES + 1):
                b = i % 2
                if i + 1 < PIECES:
                    load_piece(i + 1, 0)
                if i >= 2:
                    middle(i - 2)
                    for w in (2 * i - 4, 2 * i - 3):
                        if w < NW:
                            store_table(w)
                if i < PIECES:
                    act.wait_ge(S["turn_made"], i + 1)
                    if i >= 2:
                        act.wait_ge(S["lo_made"], i - 1)
                    a.activation(wave[:, b, :], turn[:, :, :].rearrange("p b f -> p (b f)"), ACT.Sin, scale=TWO_PI
                                 ).then_inc(S["sin_done"], 1)
                if i:
                    act.wait_ge(S["wave_scaled"], i)
                    if i >= 3:
                        act.wait_ge(parts_stored[1 - b], 16 * ((i - 1) // 2))
                    a.copy(part[:, 1 - b, 0, :], wave[:, 1 - b, :]).then_inc(S["hi_made"], 1)
                    for w in (2 * i - 2, 2 * i - 1):
                        if w < NW:
                            take_filter(w)
                if i + 1 < PIECES:
                    load_piece(i + 1, 1)
            middle(PIECES - 1)

            pairs = act.alloc_register("signed_pair")
            turns = [act.alloc_register(f"widening_turn_of_pair{q}") for q in range(2)]
            for reg in [pairs] + turns:
                act.reg_mov(reg, 1)
            act.wait_ge(S["ranges_set"], 1)
            act.wait_ge(S["half_pi_set"], 2)
            act.wait_ge(S["edges_taken"], 6)

            def signs(t, q):
                m = act.snap(pairs)
                n = act.snap(turns[q])
                for j in (2 * q, 2 * q + 1):
                    act.wait_ge(sign_used[j % 2], m)
                    a.activation(sign[:, j % 2, 0:NC1], node_no[:, 1:1 + NC1], ACT.Sign,
                                 bias=src_b[:, bass.ds(t + j, 1)]).then_inc(sign_made[j % 2], 1)
                act.wait_ge(hot_made[q], n)
                a.copy(onehot[:, 2 * q:2 * q + 2, :], onehot_bf[:, 2 * q:2 * q + 2, :]).then_inc(hot_widened[q], 1)
                act.reg_add(pairs, pairs, 1)
                act.reg_add(turns[q], turns[q], 1)

            window_regs = [act.alloc_register(n) for n in ("first_tile", "end_tile")]
            with act.Fori(0, NW) as w:
                first, end = window_range(act, w, window_regs)
                with act.Fori(first, end, TJ) as t:
                    signs(t, 0)
                    with act.If(t + 2 < end):
                        signs(t, 1)
                act.wait_ge(S["lo_made"], PIECES)
                for b in range(2):
                    act.wait_ge(parts_stored[b], 16 * through(PIECES, b))
                counted = act.snap(pairs)
                for b in range(2):
                    act.wait_ge(sign_used[b], counted)
                a.activation(cumul[:, bass.ds(w, 1), 0:NC1].rearrange("p a (b f) -> p (a b) f", b=3), psum[:, 5:8, 0:CB],
                             ACT.Identity, bias=count_bias[:, :], scale=0.5).then_inc(S["counts_flushed"], 1)
                act.wait_ge(S["window_summed"], w + 1)
                a.copy(x1[:, bass.ds(w, 1), :], bank[4].unsqueeze(1)).then_inc(S["sums_flushed"], 1)

            for w in range(NW + 1):
                if w < NW:
                    act.wait_ge(S["x1T_turned"], w + 1)
                    if w >= 2:
                        act.wait_ge(S["v_made"], w - 1)
                        act.wait_ge(S["s1_taken"], w - 1)
                    a.copy(x1T[:, w % 2, :], bank[w % 2]).then_inc(S["x1T_taken"], 1)
                if w == 0:
                    continue
                u, b = w - 1, (w - 1) % 2
                act.wait_ge(S["counts_turned"], 3 * u + 1)
                a.copy(countsT[:, 0, 0:4, u * P:(u + 1) * P], bank[6 + u % 2].rearrange("p (k f) -> p k f", f=P)
                       ).then_inc(S["counts_copied"], 1)
                act.wait_ge(S["v_made"], u + 1)
                if u:
                    act.wait_ge(S["norm_sq"], u)
                a.activation(sq[:, :], bank[4 + b][:, 0:C3], ACT.Square).then_inc(S["v_squared"], 1)
                a.copy(vv[:, u, :], bank[4 + b][:, 0:C3]).then_inc(S["v_taken"], 1)
                a.copy(vu[:, u, :], bank[2 + b][:, 0:C3]).then_inc(S["v_taken"], 1)
                if u:
                    a.activation(nrm[:, u - 1, :], ssq[:, (u - 1) % 2, :], ACT.Sqrt).then_inc(S["norm_made"], 1)
            act.wait_ge(S["norm_sq"], NW)
            a.activation(nrm[:, NW - 1, :], ssq[:, (NW - 1) % 2, :], ACT.Sqrt).then_inc(S["norm_made"], 1)
            for c, (lo, hi) in enumerate(THIRDS):
                act.wait_ge(S["z1_made"], c + 1)
                a.activation(h1T[:, lo:hi], bank[c][:, 0:hi - lo], ACT.Sigmoid, bias=bu1c[:, :]).then_inc(S["sig1_made"], 1)
            for w in range(NW + 2):
                if w < NW:
                    act.wait_ge(S["gate_made"], w + 1)
                    if w >= 2:
                        act.wait_ge(S["update_made"], 2 * (w - 1))
                    a.copy(hh[:, w % 2, :], bank[3 + w % 2][:, 0:C3]).then_inc(S["gate_taken"], 1)
                if 1 <= w <= NW:
                    act.wait_ge(S["update_made"], 2 * w)
                    a.copy(update_parts[:, w - 1, 0, :], x1[:, w - 1, :]).then_inc(S["update_hi"], 1)
                if w >= 2:
                    act.wait_ge(S["update_less_hi"], w - 1)
                    a.copy(update_parts[:, w - 2, 1, :], x1[:, w - 2, :]).then_inc(S["update_mid"], 1)
            for w in range(NW):
                act.wait_ge(S["var_made"], w + 1)
                a.activation(stat[:, w, 9:10], stat[:, w, 8:9], ACT.Sqrt).then_inc(S["std_made"], 1)

        @block.vector
        def _(dve):
            v = nc.vector
            steps = [0]

            def then(ins):
                steps[0] += 1
                ins.then_inc(S["dve_step"], 1)
                dve.wait_ge(S["dve_step"], steps[0])

            v.memset(half_pi[:, :], float(np.pi / 2)).then_inc(S["half_pi_set"], 1)
            v.memset(count_bias[:, :], E / 2 + 0.25).then_inc(S["half_pi_set"], 1)
            v.memset(ones_bf[:, :], 1.0).then_inc(S["dve_const"], 1)
            v.memset(zeros_bf[:, :], 0.0).then_inc(S["dve_const"], 1)
            dve.wait_ge(S["ld_r"], 32)
            v.tensor_scalar(tmp_a, r_r, R_CUT, None, ALU.min).then_inc(S["cos_in"], 1)
            then(v.reciprocal(coef, r_r))
            dve.wait_ge(S["cos_done"], 1)
            k = 0.5 * float(np.sqrt(np.float32(2.0 / R_CUT)))
            then(v.tensor_scalar(tmp_b, tmp_b, 1.0, k, ALU.add, ALU.mult))
            then(v.scalar_tensor_tensor(out=tmp_b, in0=r_r, scalar=R_CUT, in1=tmp_b, op0=ALU.is_lt, op1=ALU.mult))
            v.tensor_tensor(coef, tmp_b, coef, ALU.mult).then_inc(S["rc_made"], 1)
            dve.wait_ge(S["rc_made"], 1)
            then(v.tensor_copy(rc_parts[:, 1, 0], coef))
            then(v.tensor_tensor(coef, coef, rc_parts[:, 1, 0], ALU.subtract))
            then(v.tensor_copy(rc_parts[:, 1, 1], coef))
            v.tensor_tensor(rc_parts[:, 1, 2], coef, rc_parts[:, 1, 1], ALU.subtract).then_inc(S["coef_split"], 1)
            dve.wait_ge(S["ld_w2"], 64)
            for full, parts in ((w2f, w2p), (bf, bp)):
                then(v.tensor_copy(parts[:, 0, :], full))
                then(v.tensor_tensor(full, full, parts[:, 0, :], ALU.subtract))
                then(v.tensor_copy(parts[:, 1, :], full))
                v.tensor_tensor(parts[:, 2, :], full, parts[:, 1, :], ALU.subtract).then_inc(S["w2_split"], 1)
            dve.wait_ge(S["pool_const"], 7)
            then(v.tensor_scalar(pick_f, pick_i, 0.0, None, ALU.is_equal))
            then(v.scalar_tensor_tensor(out=pick_f, in0=pick_i, scalar=-float(CHUNKS), in1=pick_f, op0=ALU.is_equal, op1=ALU.add))
            v.scalar_tensor_tensor(out=pick[:, :, :], in0=pick_i, scalar=-2.0 * CHUNKS, in1=pick_f,
                                   op0=ALU.is_equal, op1=ALU.add).then_inc(S["picks_made"], 1)
            then(v.tensor_scalar(harmonic[:, :], row_i, -(CHUNKS - 1) / 2, 1.0 / CHUNKS, ALU.add, ALU.mult))
            then(v.tensor_scalar(harmonic[:, :], harmonic[:, :], MAGIC, MAGIC, ALU.add, ALU.subtract))
            v.tensor_scalar(harmonic[:, :], harmonic[:, :], 1.0, 1.0 / (2 * R_CUT), ALU.add, ALU.mult).then_inc(S["picks_made"], 1)
            v.tensor_copy(node_no[:, :], node_no_i).then_inc(S["dve_const"], 1)
            dve.wait_ge(S["ld_edges"], 16 * 8)
            v.tensor_copy(src_f, src_i).then_inc(S["edges_float"], 1)
            dve.wait_ge(S["rc_made"], 1)
            v.tensor_copy(dst_f, dst_i).then_inc(S["edges_float"], 1)
            dve.wait_ge(S["edges_float"], 2)
            then(v.tensor_copy(tmp_a, dst_hi_i))
            then(v.tensor_copy(tile_no[:, :], tile_no_i[:, :]))
            then(v.tensor_copy(win_lo[:, :], win_lo_i[:, :]))
            then(v.tensor_reduce(most[:, :], dst_f.rearrange("g (j f) -> g j f", j=TJ), AX.X, ALU.max))
            then(v.tensor_reduce(least[:, :], tmp_a.rearrange("g (j f) -> g j f", j=TJ), AX.X, ALU.min))
            then(v.tensor_scalar(to_last[:, :], tile_no[:, :], -1.0, float(NT), ALU.mult, ALU.add))
            then(v.tensor_scalar(past[:, :], tile_no[:, :], 1.0, None, ALU.add))
            for j in range(TJ):
                then(v.tensor_scalar(in_span[:, :], win_lo[:, :], float(P - 1), least[:, j:j + 1], ALU.add, ALU.is_ge))
                then(v.scalar_tensor_tensor(out=in_span[:, :], in0=win_lo[:, :], scalar=most[:, j:j + 1], in1=in_span[:, :],
                                            op0=ALU.is_le, op1=ALU.mult))
                v.tensor_scalar(span[:, j, 0, :], in_span[:, :], to_last[:, j:j + 1], -float(NT), ALU.mult,
                                ALU.add).then_inc(S["span_made"], 1)
                v.tensor_scalar(span[:, j, 1, :], in_span[:, :], past[:, j:j + 1], None, ALU.mult).then_inc(S["span_made"], 1)
                dve.wait_ge(S["span_made"], 2 * j + 2)
            dve.wait_ge(S["span_turned"], 1)
            v.tensor_reduce(span_t[:, :], bank[5][0:TJ * 2 * W11, 0:GR], AX.X, ALU.max).then_inc(S["span_max"], 1)
            dve.wait_ge(S["span_row"], 1)
            then(v.tensor_reduce(rng_f[:, :, :].rearrange("p a b -> p (a b)"),
                                 bank[5][0:1, 128:128 + TJ * 2 * W11].rearrange("p (j c) -> p c j", j=TJ), AX.X, ALU.max))
            lo_f, end_f = rng_f[0:1, 0, :], rng_f[0:1, 1, :]
            then(v.tensor_scalar(lo_f, lo_f, -1.0, float(NT - 1), ALU.mult, ALU.min))
            then(v.scalar_tensor_tensor(out=end_f, in0=lo_f, scalar=1.0, in1=end_f, op0=ALU.add, op1=ALU.max))
            then(v.scalar_tensor_tensor(out=end_f, in0=end_f, scalar=float(PACK), in1=lo_f, op0=ALU.mult, op1=ALU.add))
            v.tensor_copy(rng[:, :], end_f).then_inc(S["ranges_set"], 1)
            dve.wait_ge(S["edges_turned"], 5)

            def columns(ap):
                return ap.rearrange("p (g j) -> p j g", j=TJ)

            def turned(i):
                return bank[i][:, 0:TJ * GR].rearrange("p (j g) -> p j g", j=TJ)

            v.tensor_copy(columns(dst_c[:, :]), turned(0)).then_inc(S["edges_taken"], 1)
            v.tensor_copy(columns(src_c[:, :]), turned(1)).then_inc(S["edges_taken"], 1)
            v.tensor_scalar(columns(src_b[:, :]), turned(1), -1.0, 0.5, ALU.mult, ALU.add).then_inc(S["edges_taken"], 1)
            for c in range(3):
                v.tensor_copy(columns(ea_c[:, c]), turned(2 + c)).then_inc(S["edges_taken"], 1)
            for c, (lo, hi) in enumerate(THIRDS):
                dve.wait_ge(S["s_turned"], c + 1)
                v.tensor_copy(sT[:, lo:hi], bank[5 + c][:, 0:hi - lo]).then_inc(S["s_taken"], 1)
            for c, (lo, hi) in enumerate(THIRDS):
                dve.wait_ge(S["sig_made"], c + 1)
                v.scalar_tensor_tensor(out=hT[:, lo:hi], in0=bank[5 + c][:, 0:hi - lo], scalar=b1c[:, :], in1=hT[:, lo:hi],
                                       op0=ALU.add, op1=ALU.mult).then_inc(S["h_made"], 1)
            dve.wait_ge(S["uv_turned"], 1)
            v.tensor_copy(uT, bank[6][:, 0:C]).then_inc(S["uv_taken"], 1)
            dve.wait_ge(S["uv_made"], 1)
            v.tensor_copy(uv_sb[:, :], bank[7][:, 0:C]).then_inc(S["uv_set"], 1)
            turns_x, coef_x = psum[0:RROWS, 0:PB, 0:PW], psum[0:RROWS, PB:2 * PB, 0:PW]
            turn_row = turn.rearrange("p b f -> p (b f)")
            for i in range(PIECES + 1):
                if i < PIECES:
                    dve.wait_ge(rc_spread[0], i + 1)
                    if i:
                        dve.wait_ge(S["sin_done"], i)
                    v.tensor_scalar(turn, turns_x, harmonic[:, :], None, ALU.mult).then_inc(S["turns_taken"], 1)
                    dve.wait_ge(S["turns_taken"], i + 1)
                    then(v.tensor_scalar(nearest, turn_row, MAGIC, MAGIC, ALU.add, ALU.subtract))
                    v.tensor_tensor(turn_row, turn_row, nearest, ALU.subtract).then_inc(S["turn_made"], 1)
                if i == 0:
                    continue
                dve.wait_ge(S["sin_done"], i)
                dve.wait_ge(rc_spread[1], i)
                wv = wave[:, (i - 1) % 2, :].rearrange("p (b f) -> p b f", b=PB)
                v.tensor_tensor(wv, wv, coef_x, ALU.mult).then_inc(S["wave_scaled"], 1)
                for w in (2 * i - 2, 2 * i - 1):
                    if w < NW:
                        dve.wait_ge(S["filter_taken"], w + 1)
                        if w >= 2:
                            dve.wait_ge(table_stored[w % 2], 16 * (w // 2))
                        v.tensor_tensor(table_out[:, w % 2, 0:C3].rearrange("p (c k) -> p c k", k=3),
                                        xw[:, w, 0:C3].rearrange("p (c k) -> p c k", k=3),
                                        first_filter[:, w % 2, :].unsqueeze(2).to_broadcast((P, C, 3)),
                                        ALU.mult).then_inc(S["table_vec_made"], 1)
            b = (PIECES - 1) % 2
            dve.wait_ge(S["hi_made"], PIECES)
            dve.wait_ge(S["lo_made"], PIECES - 1)
            v.tensor_tensor(wave[:, b, :], wave[:, b, :], part[:, b, 0, :], ALU.subtract).then_inc(S["wave_less_hi"], 1)
            dve.wait_ge(S["mid_made"], PIECES)
            v.tensor_tensor(part[:, b, 2, :], wave[:, b, :], part[:, b, 1, :], ALU.subtract).then_inc(S["lo_made"], 1)

            groups = dve.alloc_register("message_group")
            turns = [dve.alloc_register(f"message_turn_of_pair{q}") for q in range(2)]
            slot_turns = [[dve.alloc_register(f"message_turn_of_slot{h}_{q}") for q in range(2)] for h in range(2)]
            for reg in [groups] + turns + slot_turns[0] + slot_turns[1]:
                dve.reg_mov(reg, 1)
            half = dve.alloc_register("half_of_messages")
            dve.reg_mov(half, 0)

            def messages(w, t, h, q):
                group, n, turn = dve.snap(groups), dve.snap(turns[q]), dve.snap(slot_turns[h][q])
                pair = slice(2 * q, 2 * q + 2)
                vec = rows[:, h, pair, 0:C3].rearrange("p j (c k) -> p j c k", k=3)
                dve.wait_ge(gathered[h][2 * q], turn * 16)
                dve.wait_ge(gathered[h][2 * q + 1], turn * 16)
                dve.wait_ge(basis_made[q], group)
                v.tensor_tensor(rows[:, h, pair, C3:TW], rows[:, h, pair, C3:TW], psum[:, pair, C:C3],
                                ALU.mult).then_inc(products_made[q], 1)
                v.tensor_tensor(vec, vec, psum[:, pair, 0:C].unsqueeze(3).to_broadcast((P, 2, C, 3)),
                                ALU.mult).then_inc(products_made[q], 1)
                for j in (2 * q, 2 * q + 1):
                    dve.wait_ge(summed[j], n)
                v.tensor_tensor(onehot_bf[:, pair, :], node_no[:, bass.ds(w * P + 2, P)].unsqueeze(1).to_broadcast((P, 2, P)),
                                dst_c[:, bass.ds(t + 2 * q, 2)].unsqueeze(2).to_broadcast((P, 2, P)),
                                ALU.is_equal).then_inc(hot_made[q], 1)
                dve.wait_ge(products_made[q], n * 2)
                for j in (2 * q, 2 * q + 1):
                    for c in range(3):
                        comp = rows[:, h, j, 0:C3].rearrange("p (c k) -> p c k", k=3)[:, :, c]
                        v.scalar_tensor_tensor(out=comp, in0=rows[:, h, j, D:TW], scalar=ea_c[:, c, bass.ds(t + j, 1)],
                                               in1=comp, op0=ALU.mult, op1=ALU.add).then_inc(msg_made[j], 1)
                dve.reg_add(turns[q], turns[q], 1)
                dve.reg_add(slot_turns[h][q], slot_turns[h][q], 1)

            def group_messages(w, t, end, h):
                messages(w, t, h, 0)
                with dve.If(t + 2 < end):
                    messages(w, t, h, 1)
                dve.reg_add(groups, groups, 1)
                dve.reg_mov(half, 1 - h)

            window_regs = [dve.alloc_register(n) for n in ("first_tile", "end_tile")]
            with dve.Fori(0, NW) as w:
                first, end = window_range(dve, w, window_regs)
                in_half = dve.snap(half)
                for h in range(2):
                    with dve.If(in_half == h):
                        with dve.Fori(first, end, 2 * TJ) as t:
                            group_messages(w, t, end, h)
                            with dve.If(t + TJ < end):
                                group_messages(w, t + TJ, end, 1 - h)

            def chunk(r, w, c, m):
                k0, k1 = 4 * c, min(NW, 4 * c + 4)
                return v.tensor_copy(countsT[:, r, k0:k1, w * P:(w + 1) * P],
                                     bank[6 + m % 2][:, 0:(k1 - k0) * P].rearrange("p (k f) -> p k f", f=P))

            def difference(out_, w):
                return v.tensor_tensor(out_, cumul[:, w, 1:NC1], cumul[:, w, 0:N], ALU.subtract)

            dve.wait_ge(S["counts_flushed"], NW + 1)
            dve.wait_ge(S["sums_flushed"], NW + 1)
            difference(counts_b[:, 0:N], 0).then_inc(S["counts_made"], 1)
            then(v.tensor_tensor(degree, cumul[:, :, N], cumul[:, :, 0], ALU.subtract))
            v.tensor_reduce(most_edges, degree, AX.X, ALU.max).then_inc(S["most_made"], 1)
            dve.wait_ge(S["most_turned"], 1)
            then(v.tensor_reduce(many_f, bank[7][0:1, 0:P], AX.X, ALU.max))
            v.tensor_scalar(many, many_f, 256.5, None, ALU.is_gt).then_inc(S["many_set"], 1)
            for w in range(NW + 1):
                if w < NW:
                    dve.wait_ge(S["x1T_taken"], w + 1)
                    v.tensor_copy(sT1[:, w * P:(w + 1) * P], x1T[:, w % 2, C3:D]).then_inc(S["s1_taken"], 1)
                    dve.wait_ge(S["counts_turned"], 3 * w + 2)
                    chunk(0, w, 1, 3 * w + 1).then_inc(S["counts_taken"], 1)
                if w:
                    u, b = w - 1, (w - 1) % 2
                    dve.wait_ge(S["v_squared"], u + 1)
                    if u >= 2:
                        dve.wait_ge(S["norm_made"], u - 1)
                    then(v.tensor_reduce(ssq[:, b, :], sq[:, :].rearrange("p (c k) -> p c k", k=3), AX.X, ALU.add))
                    v.tensor_scalar(ssq[:, b, :], ssq[:, b, :], 2.0 ** -115, None, ALU.max).then_inc(S["norm_sq"], 1)
                if w < NW:
                    dve.wait_ge(S["counts_turned"], 3 * w + 3)
                    chunk(0, w, 2, 3 * w + 2).then_inc(S["counts_taken"], 1)
                    if w + 1 < NW:
                        difference(counts_b[:, 0:N], w + 1).then_inc(S["counts_made"], 1)
            dve.wait_ge(S["many_set"], 1)
            with dve.If(dve.value_load(many[0:1, 0:1], min_val=0, max_val=1) == 1):
                for w in range(NW):
                    if w:
                        dve.wait_ge(S["rest_turned"], 3 * w)
                    difference(counts_f, w).then_inc(S["rest_step"], 1)
                    difference(counts_b[:, 0:N], w).then_inc(S["rest_step"], 1)
                    dve.wait_ge(S["rest_step"], 2 * w + 2)
                    v.tensor_tensor(rest_b[:, 0:N], counts_f, counts_b[:, 0:N], ALU.subtract).then_inc(S["rest_made"], 1)
                    for c in range(3):
                        dve.wait_ge(S["rest_turned"], 3 * w + c + 1)
                        chunk(1, w, c, c).then_inc(S["rest_taken"], 1)
            for c, (lo, hi) in enumerate(THIRDS):
                dve.wait_ge(S["norm_turned"], min(NW, (c + 1) * 4))
                v.tensor_copy(nT[:, lo:hi], bank[5 + c][:, 0:hi - lo]).then_inc(S["norm_taken"], 1)
            for c, (lo, hi) in enumerate(THIRDS):
                dve.wait_ge(S["sig1_made"], c + 1)
                v.scalar_tensor_tensor(out=h1T[:, lo:hi], in0=bank[c][:, 0:hi - lo], scalar=bu1c[:, :], in1=h1T[:, lo:hi],
                                       op0=ALU.add, op1=ALU.mult).then_inc(S["h1_made"], 1)
            for w in range(NW):
                b = w % 2
                dve.wait_ge(S["gate_taken"], w + 1)
                dve.wait_ge(S["x_residual"], w + 1)
                vec = x1[:, w, 0:C3].rearrange("p (c k) -> p c k", k=3)
                v.tensor_tensor(vec, vu[:, w, :].rearrange("p (c k) -> p c k", k=3),
                                hh[:, b, 0:C].unsqueeze(2).to_broadcast((P, C, 3)), ALU.mult).then_inc(S["update_made"], 1)
                dve.wait_ge(S["update_made"], 2 * w + 1)
                then(v.tensor_tensor(prod[:, :], x1[:, w, 0:C3], vv[:, w, :], ALU.mult))
                then(v.tensor_reduce(dot, prod[:, :].rearrange("p (c k) -> p c k", k=3), AX.X, ALU.add))
                v.tensor_tensor(x1[:, w, C3:D], dot, hh[:, b, 2 * C:C3], ALU.add).then_inc(S["update_made"], 1)

            for w in range(NW):
                res, st = y[:, w % 2, :], stat[:, w, :]
                dve.wait_ge(S["window_done"], w + 1)
                v.tensor_tensor(res, xw[:, w, :], bank[out_bank(w)], ALU.add).then_inc(S["res_made"], 1)
                dve.wait_ge(S["res_made"], w + 1)
                v.bn_stats(st[:, 0:6], res).then_inc(S["ln_stats"], 1)
                dve.wait_ge(S["ln_stats"], w + 1)
                v.bn_aggr(st[:, 6:8], st[:, 0:6]).then_inc(S["ln_mean"], 1)
                dve.wait_ge(S["ln_mean"], w + 1)
                v.tensor_scalar(st[:, 8:9], st[:, 7:8], EPS, None, ALU.add).then_inc(S["var_made"], 1)
                dve.wait_ge(S["std_made"], w + 1)
                v.reciprocal(st[:, 10:11], st[:, 9:10]).then_inc(S["ln_scale"], 1)
                dve.wait_ge(S["ln_scale"], w + 1)
                v.tensor_scalar(xw[:, w, :], res, st[:, 6:7], st[:, 10:11], ALU.subtract, ALU.mult).then_inc(S["y_made"], 1)

        @block.tensor
        def _(pe):
            mm = nc.tensor.matmul
            turn_ = nc.tensor.transpose
            for j in range(TJ):
                pe.sem_inc(summed[j], 1)
            for b in range(2):
                pe.sem_inc(sign_used[b], 1)
            pe.wait_ge(S["pool_const"], 4)
            pe.wait_ge(S["edges_float"], 2)
            ea_k = ea_r.rearrange("g (e k) -> g e k", k=3)
            for i, a in enumerate((dst_f, src_f, ea_k[:, :, 0], ea_k[:, :, 1], ea_k[:, :, 2])):
                for j in range(TJ):
                    last = turn_(bank[i][:, j * GR:(j + 1) * GR], a[:, j * P:(j + 1) * P], ident[0:GR, 0:GR])
                last.then_inc(S["edges_turned"], 1)
            pe.wait_ge(S["span_made"], 2 * TJ)
            turn_(bank[5][0:TJ * 2 * W11, 0:GR], span[:, :, :, :].rearrange("p a b c -> p (a b c)"),
                  ident[0:GR, 0:GR]).then_inc(S["span_turned"], 1)
            pe.wait_ge(S["span_max"], 1)
            turn_(bank[5][0:1, 128:128 + TJ * 2 * W11], span_t[:, :],
                  ident[0:TJ * 2 * W11, 0:TJ * 2 * W11]).then_inc(S["span_row"], 1)
            pe.wait_ge(S["ld_x"], 32)
            pe.wait_ge(S["pads_set"], 6)
            pe.wait_ge(S["ranges_set"], 1)
            for c in range(3):
                for i in range(4 * c, min(NW, 4 * c + 4)):
                    last = turn_(bank[5 + c][:, (i % 4) * P:(i % 4 + 1) * P], xw[:, i, C3:D], ident[:, :])
                last.then_inc(S["s_turned"], 1)
            pe.wait_ge(S["ld_weights"], 16 * 8)
            for c, (lo, hi) in enumerate(THIRDS):
                pe.wait_ge(S["s_taken"], c + 1)
                mm(bank[5 + c][:, 0:hi - lo], w1[:, :], sT[:, lo:hi], start=True, stop=True).then_inc(S["z_made"], 1)
            pe.wait_ge(S["h_made"], 3)
            turn_(bank[6][:, 0:C], u_sb[:, :], ident[:, :]).then_inc(S["uv_turned"], 1)
            pe.wait_ge(S["uv_taken"], 1)
            mm(bank[7][:, 0:C], uT, v_sb[:, :], start=True, stop=True).then_inc(S["uv_made"], 1)
            pe.wait_ge(S["edges_taken"], 6)
            pe.wait_ge(S["picks_made"], 2)
            pe.wait_ge(S["w2_moved"], 16 * (PARTS + 6))
            pe.wait_ge(S["dve_const"], 2)
            pe.wait_ge(S["uv_set"], 1)

            def spread(i, k):
                pe.wait_ge(rc_loaded[k], 16 * (i + 1))
                if i:
                    pe.wait_ge(S[("turns_taken", "wave_scaled")[k]], i)
                for b in range(PB):
                    last = mm(psum[0:RROWS, k * PB + b, 0:PW], pick[:, :, :].rearrange("p n c -> p (n c)"),
                              rc_piece[:, k, b * PW:(b + 1) * PW], start=True, stop=True)
                last.then_inc(rc_spread[k], 1)

            def filter_of(w):
                if w >= 2:
                    pe.wait_ge(S["table_rest_made"], w - 1)
                mm(bank[6 + w % 2][:, 0:C3], hT[:, w * P:(w + 1) * P], w3[:, :], start=True, stop=False)
                mm(bank[6 + w % 2][:, 0:C3], ones_bf[:, :], bias_parts[:, 0:C3], start=False, stop=True).then_inc(S["filter_made"], 1)

            spread(0, 0)
            for i in range(PIECES):
                spread(i, 1)
                if i + 1 < PIECES:
                    spread(i + 1, 0)
                for w in (2 * i, 2 * i + 1):
                    if w < NW:
                        filter_of(w)

            def basis(t, q):
                if q == 0:
                    last = pe.snap(t + (TJ - 1 + PIECE_TILES))
                    pe.reg_alu(pieces, pe.snap(last * RECIP), 16, ALU.logical_shift_right)
                    pe.reg_alu(pieces_had, pieces, PIECES, ALU.min)
                    pe.reg_alu(pieces_awaited, pieces_had, 1, ALU.max)
                    pe.reg_alu(moved, pieces_awaited, 16 * PARTS, ALU.mult)
                    pe.wait_ge(S["parts_moved"], moved)
                for j in (2 * q, 2 * q + 1):
                    last = mm(bank[j][:, 0:C3], radial[0:RROWS + 3, bass.ds((t + j) * P, P)], w2s[:, :], start=True, stop=True)
                last.then_inc(basis_made[q], 1)

            PIECE_TILES = PC // P
            RECIP = (1 << 16) // PIECE_TILES + 1
            assert all(n * RECIP >> 16 == n // PIECE_TILES for n in range(NT + 2 * TJ + PIECE_TILES))
            pieces, pieces_had, pieces_awaited, moved = [
                pe.alloc_register(n) for n in ("pieces_needed", "pieces_to_have", "pieces_awaited", "pieces_moved")]
            pe.wait_ge(S["table_rest_made"], NW)
            pe.wait_ge(S["wave_scaled"], PIECES)
            pairs = pe.alloc_register("counted_pair")
            turns = [pe.alloc_register(f"summed_turn_of_pair{q}") for q in range(2)]
            next_group = pe.alloc_register("next_group")
            over = pe.alloc_register("past_the_window")
            for reg in [pairs] + turns:
                pe.reg_mov(reg, 1)
            half = pe.alloc_register("half_to_sum")
            pe.reg_mov(half, 0)
            first_tile, end_tile = [pe.alloc_register(n) for n in ("first_tile", "end_tile")]
            next_regs = [pe.alloc_register(n) for n in ("next_first_tile", "next_end_tile")]
            t0, t_end = window_range(pe, 0, next_regs)
            pe.reg_mov(first_tile, t0)
            pe.reg_mov(end_tile, t_end)
            for q in range(2):
                basis(t0, q)

            def sums(h, q):
                m, n = pe.snap(pairs), pe.snap(turns[q])
                pe.wait_ge(hot_made[q], n)
                for j in (2 * q, 2 * q + 1):
                    pe.wait_ge(sign_made[j % 2], m)
                    for b in range(3):
                        last = mm(bank[5 + b][:, 0:CB], onehot_bf[:, j, :], sign[:, j % 2, b * CB:(b + 1) * CB],
                                  start=False, stop=True, skip_group_check=True)
                    last.then_inc(sign_used[j % 2], 1)
                if q == 0:
                    pe.wait_ge(products_made[q], n * 2)
                    basis(pe.snap(next_group, min_val=0, max_val=NT - 1), q)
                pe.wait_ge(hot_widened[q], n)
                for j in (2 * q, 2 * q + 1):
                    pe.wait_ge(msg_made[j], n * 3)
                    mm(bank[4], onehot[:, j, :], rows[:, bass.ds(h, 1), j, 0:D].rearrange("p h f -> p (h f)"), start=False,
                       stop=True, skip_group_check=True).then_inc(summed[j], 1)
                pe.reg_add(pairs, pairs, 1)
                pe.reg_add(turns[q], turns[q], 1)

            with pe.Fori(0, NW) as w:
                first = pe.snap(first_tile, min_val=0, max_val=NT - 1)
                end = pe.snap(end_tile, min_val=1, max_val=NT)
                first_next, end_next = window_range(pe, w + 1, next_regs)
                pe.reg_mov(first_tile, first_next)
                pe.reg_mov(end_tile, end_next)
                pe.wait_ge(S["counts_flushed"], w + 1)
                for b in range(3):
                    mm(bank[5 + b][:, 0:CB], zeros_bf[:, 0:P], zeros_bf[:, 0:CB], start=True, stop=True, skip_group_check=True)
                pe.wait_ge(S["sums_flushed"], w + 1)
                mm(bank[4], zeros_bf[:, 0:P], zeros_bf[:, :], start=True, stop=True, skip_group_check=True)
                with pe.Fori(first, end, TJ) as t:
                    pe.reg_alu(over, t + TJ, end, ALU.is_ge)
                    o = pe.snap(over)
                    pe.reg_mov(next_group, pe.snap(t + TJ + o * (first_next - t - TJ), min_val=0, max_val=NT - 1))
                    h = pe.snap(half, min_val=0, max_val=1)
                    sums(h, 0)
                    with pe.If(t + 2 < end):
                        sums(h, 1)
                    basis(pe.snap(next_group, min_val=0, max_val=NT - 1), 1)
                    pe.reg_alu(half, 1, half, ALU.subtract)
                mm(bank[4], zeros_bf[:, 0:P], zeros_bf[:, :], start=False, stop=True, skip_group_check=True
                   ).then_inc(S["window_summed"], 1)

            def turn_chunk(counts, c, m):
                for k in range(4 * c, min(NW, 4 * c + 4)):
                    last = mm(bank[6 + m % 2][:, (k % 4) * P:(k % 4 + 1) * P], counts[:, k * P:(k + 1) * P], ident_bf,
                              start=True, stop=True)
                return last

            def turn_x1(w):
                pe.wait_ge(S["node_added"], w + 1)
                if w >= 2:
                    pe.wait_ge(S["x1T_taken"], w - 1)
                for i in range(4):
                    last = turn_(bank[w % 2][:, i * P:(i + 1) * P], x1[:, w, i * P:(i + 1) * P], ident[:, :])
                last.then_inc(S["x1T_turned"], 1)

            turn_x1(0)
            pe.wait_ge(S["most_made"], 1)
            turn_(bank[7][0:1, 0:P], most_edges, ident[:, :]).then_inc(S["most_turned"], 1)
            pe.wait_ge(S["many_set"], 1)
            pe.wait_ge(S["stage3_const"], 3)
            for w in range(NW):
                b = w % 2
                if w + 1 < NW:
                    turn_x1(w + 1)
                pe.wait_ge(S["counts_made"], w + 1)
                for c in (0, 1):
                    if w:
                        pe.wait_ge(S["counts_taken"], 2 * w - 1 + c)
                    turn_chunk(counts_b, c, 3 * w + c).then_inc(S["counts_turned"], 1)
                pe.wait_ge(S["x1T_taken"], w + 1)
                if w >= 2:
                    pe.wait_ge(S["v_taken"], 2 * (w - 1))
                for i in range(3):
                    lhs = x1T[:, b, i * C:(i + 1) * C]
                    mm(bank[2 + b][:, i * C:(i + 1) * C], lhs, u_sb[:, :], start=True, stop=True)
                    last = mm(bank[4 + b][:, i * C:(i + 1) * C], lhs, uv_sb[:, :], start=True, stop=True)
                last.then_inc(S["v_made"], 1)
                pe.wait_ge(S["counts_copied"], w + 1)
                turn_chunk(counts_b, 2, 3 * w + 2).then_inc(S["counts_turned"], 1)
            def hidden(c, first):
                lo, hi = THIRDS[c]
                return mm(bank[c][:, 0:hi - lo], wu1[:, 0 if not first else 1, :], (sT1 if first else nT)[:, lo:hi],
                          start=first, stop=not first)

            pe.wait_ge(S["s1_taken"], NW)
            pe.wait_ge(S["x1T_taken"], NW)
            for c in (0, 1):
                hidden(c, True)
            pe.wait_ge(S["v_taken"], 2 * NW)
            hidden(2, True)
            pe.wait_ge(S["counts_taken"], 2 * NW)
            pe.wait_ge(S["counts_copied"], NW)
            many_edges = pe.value_load(many[0:1, 0:1], min_val=0, max_val=1)
            with pe.If(many_edges == 1):
                for w in range(NW):
                    pe.wait_ge(S["rest_made"], w + 1)
                    for c in range(3):
                        if w or c == 2:
                            pe.wait_ge(S["rest_taken"], 3 * w + (c == 2))
                        turn_chunk(rest_b, c, c).then_inc(S["rest_turned"], 1)
                pe.wait_ge(S["rest_taken"], 3 * NW)
            for w in range(NW):
                pe.wait_ge(S["norm_made"], w + 1)
                turn_(bank[5 + w // 4][:, (w % 4) * P:(w % 4 + 1) * P], nrm[:, w, :], ident[:, :]).then_inc(S["norm_turned"], 1)
            for c in range(3):
                pe.wait_ge(S["norm_taken"], c + 1)
                hidden(c, False).then_inc(S["z1_made"], 1)

            def second_messages(d, s, r=0):
                n = P if s < NFULL else NTAIL
                for k in range(3):
                    last = mm(bank[out_bank(d)], countsT[0:n, r, s, d * P:(d + 1) * P], update_parts[0:n, s, k, :],
                              start=(r == 0 and s == 0 and k == 0), stop=(r == 0 and s == NW - 1 and k == 2))
                return last

            def rest_and_last(d):
                with pe.If(many_edges == 1):
                    for s in range(NW):
                        second_messages(d, s, 1)
                second_messages(d, NW - 1).then_inc(S["window_done"], 1)

            pe.wait_ge(S["norm_taken"], 3)
            LAG = 4
            for w in range(NW + LAG):
                if w < NW:
                    pe.wait_ge(S["h1_made"], w // 4 + 1)
                    if w >= 2:
                        pe.wait_ge(S["gate_taken"], w - 1)
                    mm(bank[3 + w % 2][:, 0:C3], h1T[:, w * P:(w + 1) * P], wu2[:, :], start=True, stop=False)
                    mm(bank[3 + w % 2][:, 0:C3], ones_bf[:, :], bias_parts[:, C3:2 * C3], start=False, stop=True).then_inc(S["gate_made"], 1)
                if w >= LAG:
                    pe.wait_ge(S["update_split"], w - LAG + 1)
                    for d in range(EARLY):
                        if w - LAG < NW - 1:
                            second_messages(d, w - LAG)
                        else:
                            rest_and_last(d)
            pe.wait_ge(S["gate_taken"], NW)
            for d in range(EARLY, NW):
                if d >= EARLY + 4:
                    pe.wait_ge(S["res_made"], d - 3)
                for s in range(NW - 1):
                    second_messages(d, s)
                rest_and_last(d)


_INS = ['x', 'src', 'dst', 'edge_attr_3', 'edge_weight', 'L0_gnn_W1', 'L0_gnn_b1', 'L0_gnn_W2', 'L0_gnn_b2',
        'L0_gnn_W3', 'L0_gnn_b3', 'L0_gnn_U', 'L0_gnn_V', 'L0_gnn_Wu1', 'L0_gnn_bu1', 'L0_gnn_Wu2', 'L0_gnn_bu2']


def kernel(**inputs):
    import concourse.bacc as bacc
    from concourse.bass_utils import run_bass_kernel_spmd

    nc = bacc.Bacc("TRN2", target_bir_lowering=False, num_devices=1)
    arrays, args = {}, []
    for name in _INS:
        a = np.ascontiguousarray(inputs[name])
        arrays[f"in_{name}"] = a
        args.append(nc.dram_tensor(f"in_{name}", a.shape, mybir.dt.from_np(a.dtype), kind="ExternalInput").ap())
    out = nc.dram_tensor("out", inputs["x"].shape, F32, kind="ExternalOutput").ap()
    build(nc, *args, out)
    r = run_bass_kernel_spmd(nc, [arrays], core_ids=[0])
    return r.results[0]["out"]
```
